# Optimizing a Trainium2 kernel written in Bass

```python
import numpy as np
import jax
import jax.numpy as jnp

def _softmax(x, axis=-1):
    return jax.nn.softmax(x, axis=axis)

def _gelu(x):
    return jax.nn.gelu(x, approximate=True)

def _silu(x):
    return jax.nn.silu(x)

def _sigmoid(x):
    return jax.nn.sigmoid(x)

def _layernorm(x, axis=-1, eps=1e-05):
    m = jnp.mean(x, axis=axis, keepdims=True)
    v = jnp.var(x, axis=axis, keepdims=True)
    return (x - m) / jnp.sqrt(v + eps)

def _scatter_add(tgt, idx, src, axis=0):
    return tgt.at[idx].add(src)

def _segment_sum(src, seg, n):
    return jax.ops.segment_sum(src, seg, n)
kernel_name = 'mk_perceiver_d4_seqx_r4_58e76d'

def setup_inputs(seed: int=0):
    np.random.seed(seed)
    _w = jnp.asarray

    def _rec_inputs():
        import jax
        import jax.numpy as jnp
        _rk = jax.random.key(seed)
        x = -0.0005146 + 1 * jax.random.normal(jax.random.fold_in(_rk, 1), (8, 64, 256), jnp.float32)
        _lenS = 64 - jax.random.randint(jax.random.fold_in(_rk, 7), (8,), 0, max(1, 64 // 4) + 1, jnp.int32)
        _lenS2 = 1601 - jax.random.randint(jax.random.fold_in(_rk, 8), (8,), 0, max(1, 1601 // 4) + 1, jnp.int32)
        _ctx_1024P = jax.random.normal(jax.random.fold_in(_rk, 11), (8, 16, 256), jnp.float32)
        _ctx_1024c = jax.random.dirichlet(jax.random.fold_in(_rk, 511), 0.3 * jnp.ones((16,), jnp.float32), (8, 1601))
        _ctx_1024t = jnp.einsum('bsk,bkd->bsd', _ctx_1024c, _ctx_1024P)
        _ctx_1024t = _ctx_1024t * jax.lax.rsqrt(jnp.mean(jnp.square(_ctx_1024t)) + 1e-12) * 0.953939
        ctx_1024 = -0.000392918 + 0.999932 * (_ctx_1024t + 0.3 * jax.random.normal(jax.random.fold_in(_rk, 611), (8, 1601, 256), jnp.float32))
        _validS = jnp.arange(64)[None, :] < _lenS[:, None]
        _validS2 = jnp.arange(1601)[None, :] < _lenS2[:, None]
        _causal = jnp.tril(jnp.ones((64, 64), dtype=bool))
        mask_BxS2_bf1 = jnp.ones((8, 1601), dtype=bool)
        mask_1x1xSxS2_fk1 = jnp.where(jnp.broadcast_to(_validS2[0:1, None, None, :], (1, 1, 64, 1601)), 1.0, 0.0).astype(jnp.float32)
        mask_BxSxS2_ff0 = jnp.where(jnp.ones((8, 64, 1601), dtype=bool), 0.0, -1000000000.0).astype(jnp.float32)
        return (x, ctx_1024, mask_BxS2_bf1, mask_1x1xSxS2_fk1, mask_BxSxS2_ff0)
    x, ctx_1024, mask_BxS2_bf1, mask_1x1xSxS2_fk1, mask_BxSxS2_ff0 = _rec_inputs()

    def _L0_xattn_setup():
        import jax, jax.numpy as jnp
        import numpy as np
        DIM = 256
        DIM_LATENT = 256
        DIM_HEAD = 64
        HEADS = 16
        INNER = HEADS * DIM_HEAD

        def layernorm(x, g, b, eps=1e-05):
            m = jnp.mean(x, axis=-1, keepdims=True)
            v = jnp.mean((x - m) ** 2, axis=-1, keepdims=True)
            return (x - m) / jnp.sqrt(v + eps) * g + b

        def rmsnorm(x, gamma, eps=1e-08):
            n = jnp.linalg.norm(x, axis=-1, keepdims=True) * x.shape[-1] ** (-0.5)
            return x / jnp.maximum(n, eps) * gamma
        key = jax.random.key(seed)
        ks = jax.random.split(key, 8)
        b, n, m = (4, 1024, 128)
        x = jax.random.normal(ks[0], (b, n, DIM), dtype=jnp.float32)
        latents = jax.random.normal(ks[1], (b, m, DIM_LATENT), dtype=jnp.float32)
        mask = jnp.ones((b, n), dtype=bool)
        s = 0.02
        return {'x': x, 'latents': latents, 'mask': mask, 'ln_x_g': jnp.ones((DIM,), jnp.float32), 'ln_x_b': jnp.zeros((DIM,), jnp.float32), 'ln_l_g': jnp.ones((DIM_LATENT,), jnp.float32), 'ln_l_b': jnp.zeros((DIM_LATENT,), jnp.float32), 'qn_g': jnp.ones((DIM_HEAD,), jnp.float32), 'kn_g': jnp.ones((DIM_HEAD,), jnp.float32), 'Wq': jax.random.normal(ks[2], (DIM_LATENT, INNER), jnp.float32) * s, 'Wkv': jax.random.normal(ks[3], (DIM, 2 * INNER), jnp.float32) * s, 'Wout': jax.random.normal(ks[4], (INNER, DIM_LATENT), jnp.float32) * s, 'bout': jnp.zeros((DIM_LATENT,), jnp.float32)}
    _L0_xattn_all = _L0_xattn_setup()
    _L0_xattn_in = {k: v for k, v in _L0_xattn_all.items() if k in ('ln_x_g', 'ln_x_b', 'ln_l_g', 'ln_l_b', 'qn_g', 'kn_g', 'Wq', 'Wkv', 'Wout', 'bout')}
    del _L0_xattn_all

    def _L0_attn_setup():
        import jax, jax.numpy as jnp
        import numpy as np
        D_MODEL = 256
        N_HEADS = 16
        WINDOW = 64
        SEQ = 1024
        BATCH = 1
        NEG_INF = -1e+30
        key = jax.random.key(seed)
        ks = jax.random.split(key, 5)
        scale = 0.02
        inp = {'x': jax.random.normal(ks[0], (BATCH, SEQ, D_MODEL), jnp.float32)}
        for i, name in enumerate(['Wq', 'Wk', 'Wv', 'Wo']):
            inp[name] = jax.random.normal(ks[1 + i], (D_MODEL, D_MODEL), jnp.float32) * scale
        for name in ['bq', 'bk', 'bv', 'bo']:
            inp[name] = jnp.zeros((D_MODEL,), jnp.float32)
        return inp
    _L0_attn_all = _L0_attn_setup()
    _L0_attn_in = {k: v for k, v in _L0_attn_all.items() if k in ('Wq', 'bq', 'Wk', 'bk', 'Wv', 'bv', 'Wo', 'bo')}
    del _L0_attn_all

    def _L0_ffn_setup():
        import jax, jax.numpy as jnp
        import numpy as np
        key = jax.random.key(seed)
        ks = jax.random.split(key, 5)
        B, T, D, E = (4, 512, 256, 8)
        inputs = jax.random.normal(ks[0], (B, T, D), dtype=jnp.float32)
        Wr = jax.random.normal(ks[1], (D, E), dtype=jnp.float32) * 0.02
        br = jnp.zeros((E,), dtype=jnp.float32)
        W1 = jax.random.normal(ks[2], (E, D, D), dtype=jnp.float32) * 0.02
        b1 = jnp.zeros((E, D), dtype=jnp.float32)
        W2 = jax.random.normal(ks[3], (E, D, D), dtype=jnp.float32) * 0.02
        b2 = jnp.zeros((E, D), dtype=jnp.float32)
        return {'inputs': inputs, 'Wr': Wr, 'br': br, 'W1': W1, 'b1': b1, 'W2': W2, 'b2': b2}
    _L0_ffn_all = _L0_ffn_setup()
    _L0_ffn_in = {k: v for k, v in _L0_ffn_all.items() if k in ('Wr', 'br', 'W1', 'b1', 'W2', 'b2')}
    del _L0_ffn_all

    def _L1_xattn_setup():
        import jax, jax.numpy as jnp
        import numpy as np
        D_MODEL = 256
        NUM_HEADS = 16
        DEPTH = D_MODEL // NUM_HEADS
        B, S = (4, 512)

        def _split_heads(x):
            b, s, _ = x.shape
            return x.reshape(b, s, NUM_HEADS, DEPTH).transpose(0, 2, 1, 3)
        key = jax.random.key(seed)
        ks = jax.random.split(key, 12)
        scale = 1.0 / np.sqrt(D_MODEL)
        inp = {'q': jax.random.normal(ks[0], (B, S, D_MODEL), jnp.float32), 'k': jax.random.normal(ks[1], (B, S, D_MODEL), jnp.float32), 'v': jax.random.normal(ks[2], (B, S, D_MODEL), jnp.float32), 'mask': jnp.triu(jnp.ones((S, S), jnp.float32), k=1)[None, None, :, :], 'wq': jax.random.normal(ks[3], (D_MODEL, D_MODEL), jnp.float32) * scale, 'bq': jnp.zeros((D_MODEL,), jnp.float32), 'wk': jax.random.normal(ks[4], (D_MODEL, D_MODEL), jnp.float32) * scale, 'bk': jnp.zeros((D_MODEL,), jnp.float32), 'wv': jax.random.normal(ks[5], (D_MODEL, D_MODEL), jnp.float32) * scale, 'bv': jnp.zeros((D_MODEL,), jnp.float32), 'wo': jax.random.normal(ks[6], (D_MODEL, D_MODEL), jnp.float32) * scale, 'bo': jnp.zeros((D_MODEL,), jnp.float32)}
        return inp
    _L1_xattn_all = _L1_xattn_setup()
    _L1_xattn_in = {k: v for k, v in _L1_xattn_all.items() if k in ('wq', 'bq', 'wk', 'bk', 'wv', 'bv', 'wo', 'bo')}
    del _L1_xattn_all

    def _L1_attn_setup():
        import jax, jax.numpy as jnp
        import numpy as np

        def _layernorm(x, g, b, eps=1e-05):
            m = x.mean(-1, keepdims=True)
            v = x.var(-1, keepdims=True)
            return (x - m) * jax.lax.rsqrt(v + eps) * g + b

        def _mamba(x, in_w, conv_w, conv_b, xproj_w, dt_w, dt_b, A_log, D, out_w):
            Bsz, L, _ = x.shape
            d_state = A_log.shape[1]
            dt_rank = dt_w.shape[1]
            d_conv = conv_w.shape[1]
            u, z = jnp.split(x @ in_w.T, 2, axis=-1)
            u_pad = jnp.pad(u, ((0, 0), (d_conv - 1, 0), (0, 0)))
            u = sum((u_pad[:, k:k + L, :] * conv_w[:, k] for k in range(d_conv))) + conv_b
            u = jax.nn.silu(u)
            dbc = u @ xproj_w.T
            dt = jax.nn.softplus(dbc[..., :dt_rank] @ dt_w.T + dt_b)
            Bm = dbc[..., dt_rank:dt_rank + d_state]
            Cm = dbc[..., dt_rank + d_state:]
            A = -jnp.exp(A_log)
            dA = jnp.exp(dt[..., None] * A)
            dBu = (dt * u)[..., None] * Bm[:, :, None, :]

            def step(h, inp):
                dA_t, dBu_t, C_t = inp
                h = dA_t * h + dBu_t
                return (h, jnp.einsum('bdn,bn->bd', h, C_t))
            h0 = jnp.zeros((Bsz, u.shape[-1], d_state), x.dtype)
            _, ys = jax.lax.scan(step, h0, (dA.swapaxes(0, 1), dBu.swapaxes(0, 1), Cm.swapaxes(0, 1)))
            y = ys.swapaxes(0, 1) + u * D
            return y * jax.nn.silu(z) @ out_w.T
        key = jax.random.key(seed)
        ks = jax.random.split(key, 3)
        d_model, d_state, d_conv, d_inner, dt_rank = (256, 16, 4, 512, 64)
        B, L = (2, 256)

        def mk(k, shape, s=0.02):
            return jax.random.normal(k, shape, jnp.float32) * s

        def mamba_params(kb):
            k = jax.random.split(kb, 6)
            return {'in_w': mk(k[0], (2 * d_inner, d_model)), 'conv_w': mk(k[1], (d_inner, d_conv), 0.2), 'conv_b': jnp.zeros((d_inner,), jnp.float32), 'xproj_w': mk(k[2], (dt_rank + 2 * d_state, d_inner)), 'dt_w': mk(k[3], (d_inner, dt_rank), 0.1), 'dt_b': jnp.full((d_inner,), -4.0, jnp.float32) + mk(k[4], (d_inner,), 0.5), 'Alog': jnp.log(jnp.tile(jnp.arange(1, d_state + 1, dtype=jnp.float32), (d_inner, 1))), 'D': jnp.ones((d_inner,), jnp.float32), 'out_w': mk(k[5], (d_model, d_inner))}
        pf = mamba_params(ks[0])
        pb = mamba_params(ks[1])
        inp = {'x': jax.random.normal(ks[2], (B, L, d_model), jnp.float32), 'ln_g': jnp.ones((d_model,), jnp.float32), 'ln_b': jnp.zeros((d_model,), jnp.float32)}
        for pre, p in (('f_', pf), ('b_', pb)):
            for nm, v in p.items():
                inp[pre + nm] = v
        return inp
    _L1_attn_all = _L1_attn_setup()
    _L1_attn_in = {k: v for k, v in _L1_attn_all.items() if k in ('ln_g', 'ln_b', 'f_in_w', 'f_conv_w', 'f_conv_b', 'f_xproj_w', 'f_dt_w', 'f_dt_b', 'f_Alog', 'f_D', 'f_out_w', 'b_in_w', 'b_conv_w', 'b_conv_b', 'b_xproj_w', 'b_dt_w', 'b_dt_b', 'b_Alog', 'b_D', 'b_out_w')}
    del _L1_attn_all

    def _L1_ffn_setup():
        import jax, jax.numpy as jnp
        import numpy as np
        ALPHA = 1.702
        LIMIT = 7.0
        TOPK = 2
        D, I, E = (256, 512, 8)
        B, S = (2, 512)

        def swiglu(x):
            g = x[..., ::2]
            l = x[..., 1::2]
            g = jnp.minimum(g, LIMIT)
            l = jnp.clip(l, -LIMIT, LIMIT)
            return g * jax.nn.sigmoid(ALPHA * g) * (l + 1.0)
        key = jax.random.key(seed)
        ks = jax.random.split(key, 16)
        sc = 0.02
        n = lambda k, shape, s=sc: jax.random.normal(k, shape, dtype=jnp.float32) * s
        return {'x': jax.random.normal(ks[0], (B, S, D), dtype=jnp.float32), 'gate_w': n(ks[1], (E, D)), 'gate_b': n(ks[2], (E,)), 'w1': n(ks[3], (E, D, 2 * I)), 'b1': n(ks[4], (E, 2 * I)), 'w3': n(ks[5], (E, D, 2 * I)), 'b3': n(ks[6], (E, 2 * I)), 'w2': n(ks[7], (E, I, D)), 'b2': n(ks[8], (E, D)), 'sw1': n(ks[9], (D, 2 * I)), 'sb1': n(ks[10], (2 * I,)), 'sw3': n(ks[11], (D, 2 * I)), 'sb3': n(ks[12], (2 * I,)), 'sw2': n(ks[13], (I, D)), 'sb2': n(ks[14], (D,))}
    _L1_ffn_all = _L1_ffn_setup()
    _L1_ffn_in = {k: v for k, v in _L1_ffn_all.items() if k in ('gate_w', 'gate_b', 'w1', 'b1', 'w3', 'b3', 'w2', 'b2', 'sw1', 'sb1', 'sw3', 'sb3', 'sw2', 'sb2')}
    del _L1_ffn_all

    def _L2_xattn_setup():
        import jax, jax.numpy as jnp
        import numpy as np
        B, S, D, H = (4, 512, 256, 256)
        key = jax.random.key(seed)
        k1, k2, k3, k4, k5, k6 = jax.random.split(key, 6)
        return {'x1': jax.random.normal(k1, (B, S, D), dtype=jnp.float32), 'x2': jax.random.normal(k2, (B, S, D), dtype=jnp.float32), 'x3': jax.random.normal(k3, (B, S, D), dtype=jnp.float32), 'mask': jnp.zeros((B, S, S), dtype=jnp.float32), 'Wq': jax.random.normal(k4, (H, D), dtype=jnp.float32) * (1.0 / np.sqrt(D)), 'Wk': jax.random.normal(k5, (H, D), dtype=jnp.float32) * (1.0 / np.sqrt(D)), 'Wv': jax.random.normal(k6, (H, D), dtype=jnp.float32) * (1.0 / np.sqrt(D))}
    _L2_xattn_all = _L2_xattn_setup()
    _L2_xattn_in = {k: v for k, v in _L2_xattn_all.items() if k in ('Wq', 'Wk', 'Wv')}
    del _L2_xattn_all

    def _L2_attn_setup():
        import jax, jax.numpy as jnp
        import numpy as np
        BATCH, SEQ, D_MODEL = (4, 512, 256)
        D_STATE, D_CONV = (16, 4)

        def _silu(u):
            return u * jax.nn.sigmoid(u)
        key = jax.random.key(seed)
        ks = jax.random.split(key, 6)
        s = 0.02
        x = jax.random.normal(ks[0], (BATCH, SEQ, D_MODEL), jnp.float32)
        in_proj_w = jax.random.normal(ks[1], (2 * D_MODEL, D_MODEL), jnp.float32) * s
        conv_w = jax.random.normal(ks[2], (D_MODEL, D_CONV), jnp.float32) * s
        conv_b = jax.random.normal(ks[3], (D_MODEL,), jnp.float32) * s
        x_proj_w = jax.random.normal(ks[4], (2 * D_STATE + 1, D_MODEL), jnp.float32) * s
        A_log = jnp.log(jnp.broadcast_to(jnp.arange(1, D_STATE + 1, dtype=jnp.float32), (D_MODEL, D_STATE)))
        D_param = jnp.ones((D_MODEL,), jnp.float32)
        out_proj_w = jax.random.normal(ks[5], (D_MODEL, D_MODEL), jnp.float32) * s
        return {'x': x, 'in_proj_w': in_proj_w, 'conv_w': conv_w, 'conv_b': conv_b, 'x_proj_w': x_proj_w, 'A_log': A_log, 'D_param': D_param, 'out_proj_w': out_proj_w}
    _L2_attn_all = _L2_attn_setup()
    _L2_attn_in = {k: v for k, v in _L2_attn_all.items() if k in ('in_proj_w', 'conv_w', 'conv_b', 'x_proj_w', 'A_log', 'D_param', 'out_proj_w')}
    del _L2_attn_all

    def _L2_ffn_setup():
        import jax, jax.numpy as jnp
        import numpy as np
        K = 2
        key = jax.random.key(seed)
        ks = jax.random.split(key, 7)
        B, S, D, E = (2, 512, 256, 8)
        H = 4 * D
        sd = 1.0 / np.sqrt(D)
        sh = 1.0 / np.sqrt(H)
        return {'x': jax.random.normal(ks[0], (B, S, D), jnp.float32), 'Wr': jax.random.normal(ks[1], (D, E), jnp.float32) * sd, 'br': jax.random.normal(ks[2], (E,), jnp.float32) * sd, 'W1': jax.random.normal(ks[3], (E, D, H), jnp.float32) * sd, 'b1': jax.random.normal(ks[4], (E, H), jnp.float32) * sd, 'W2': jax.random.normal(ks[5], (E, H, D), jnp.float32) * sh, 'b2': jax.random.normal(ks[6], (E, D), jnp.float32) * sh}
    _L2_ffn_all = _L2_ffn_setup()
    _L2_ffn_in = {k: v for k, v in _L2_ffn_all.items() if k in ('Wr', 'br', 'W1', 'b1', 'W2', 'b2')}
    del _L2_ffn_all

    def _L3_xattn_setup():
        import jax, jax.numpy as jnp
        import numpy as np
        B, T, C, H = (4, 1024, 256, 16)
        D = C // H

        def _heads(t):
            b, n, c = t.shape
            return t.reshape(b, n, H, D).transpose(0, 2, 1, 3)
        key = jax.random.key(seed)
        ks = jax.random.split(key, 10)
        s = 1.0 / np.sqrt(C)
        return {'x': jax.random.normal(ks[0], (B, T, C), jnp.float32), 'y': jax.random.normal(ks[1], (B, T, C), jnp.float32), 'Wq': jax.random.normal(ks[2], (C, C), jnp.float32) * s, 'bq': jnp.zeros((C,), jnp.float32), 'Wk': jax.random.normal(ks[3], (C, C), jnp.float32) * s, 'bk': jnp.zeros((C,), jnp.float32), 'Wv': jax.random.normal(ks[4], (C, C), jnp.float32) * s, 'bv': jnp.zeros((C,), jnp.float32), 'Wp': jax.random.normal(ks[5], (C, C), jnp.float32) * s, 'bp': jnp.zeros((C,), jnp.float32)}
    _L3_xattn_all = _L3_xattn_setup()
    _L3_xattn_in = {k: v for k, v in _L3_xattn_all.items() if k in ('Wq', 'bq', 'Wk', 'bk', 'Wv', 'bv', 'Wp', 'bp')}
    del _L3_xattn_all

    def _L3_attn_setup():
        import jax, jax.numpy as jnp
        import numpy as np
        import math
        B, S, D = (4, 512, 256)
        H, KV = (16, 4)
        HD = D // H
        GROUPS = H // KV

        def _alibi_slopes(n):
            start = 2.0 ** (-2.0 ** (-(math.log2(n) - 3)))
            return np.array([start * start ** i for i in range(n)], dtype=np.float32)
        key = jax.random.key(seed)
        ks = jax.random.split(key, 5)
        sc = 0.02
        return {'x': jax.random.normal(ks[0], (B, S, D), jnp.float32), 'Wq': jax.random.normal(ks[1], (D, H * HD), jnp.float32) * sc, 'Wk': jax.random.normal(ks[2], (D, KV * HD), jnp.float32) * sc, 'Wv': jax.random.normal(ks[3], (D, KV * HD), jnp.float32) * sc, 'Wo': jax.random.normal(ks[4], (H * HD, D), jnp.float32) * sc}
    _L3_attn_all = _L3_attn_setup()
    _L3_attn_in = {k: v for k, v in _L3_attn_all.items() if k in ('Wq', 'Wk', 'Wv', 'Wo')}
    del _L3_attn_all

    def _L3_ffn_setup():
        import jax, jax.numpy as jnp
        import numpy as np
        NUM_HEADS = 16
        TOP_K = 2
        key = jax.random.key(seed)
        ks = jax.random.split(key, 5)
        B, S, D, E = (4, 512, 256, 8)
        scale = 0.02
        return {'x': jax.random.normal(ks[0], (B, S, D), dtype=jnp.float32), 'W_qkv': jax.random.normal(ks[1], (D, 3 * D), dtype=jnp.float32) * scale, 'b_qkv': jnp.zeros((3 * D,), dtype=jnp.float32), 'W_gate': jax.random.normal(ks[2], (D, E), dtype=jnp.float32) * scale, 'b_gate': jnp.zeros((E,), dtype=jnp.float32), 'W_experts': jax.random.normal(ks[3], (E, D, D), dtype=jnp.float32) * scale, 'b_experts': jnp.zeros((E, D), dtype=jnp.float32)}
    _L3_ffn_all = _L3_ffn_setup()
    _L3_ffn_in = {k: v for k, v in _L3_ffn_all.items() if k in ('W_qkv', 'b_qkv', 'W_gate', 'b_gate', 'W_experts', 'b_experts')}
    del _L3_ffn_all
    return {'x': x, 'ctx_1024': ctx_1024, 'mask_BxS2_bf1': mask_BxS2_bf1, 'mask_1x1xSxS2_fk1': mask_1x1xSxS2_fk1, 'mask_BxSxS2_ff0': mask_BxSxS2_ff0, 'L0_xattn_ln_x_g': _L0_xattn_in['ln_x_g'], 'L0_xattn_ln_x_b': _L0_xattn_in['ln_x_b'], 'L0_xattn_ln_l_g': _L0_xattn_in['ln_l_g'], 'L0_xattn_ln_l_b': _L0_xattn_in['ln_l_b'], 'L0_xattn_qn_g': _L0_xattn_in['qn_g'], 'L0_xattn_kn_g': _L0_xattn_in['kn_g'], 'L0_xattn_Wq': _L0_xattn_in['Wq'], 'L0_xattn_Wkv': _L0_xattn_in['Wkv'], 'L0_xattn_Wout': _L0_xattn_in['Wout'], 'L0_xattn_bout': _L0_xattn_in['bout'], 'L0_attn_Wq': _L0_attn_in['Wq'], 'L0_attn_bq': _L0_attn_in['bq'], 'L0_attn_Wk': _L0_attn_in['Wk'], 'L0_attn_bk': _L0_attn_in['bk'], 'L0_attn_Wv': _L0_attn_in['Wv'], 'L0_attn_bv': _L0_attn_in['bv'], 'L0_attn_Wo': _L0_attn_in['Wo'], 'L0_attn_bo': _L0_attn_in['bo'], 'L0_ffn_Wr': _L0_ffn_in['Wr'], 'L0_ffn_br': _L0_ffn_in['br'], 'L0_ffn_W1': _L0_ffn_in['W1'], 'L0_ffn_b1': _L0_ffn_in['b1'], 'L0_ffn_W2': _L0_ffn_in['W2'], 'L0_ffn_b2': _L0_ffn_in['b2'], 'L1_xattn_wq': _L1_xattn_in['wq'], 'L1_xattn_bq': _L1_xattn_in['bq'], 'L1_xattn_wk': _L1_xattn_in['wk'], 'L1_xattn_bk': _L1_xattn_in['bk'], 'L1_xattn_wv': _L1_xattn_in['wv'], 'L1_xattn_bv': _L1_xattn_in['bv'], 'L1_xattn_wo': _L1_xattn_in['wo'], 'L1_xattn_bo': _L1_xattn_in['bo'], 'L1_attn_ln_g': _L1_attn_in['ln_g'], 'L1_attn_ln_b': _L1_attn_in['ln_b'], 'L1_attn_f_in_w': _L1_attn_in['f_in_w'], 'L1_attn_f_conv_w': _L1_attn_in['f_conv_w'], 'L1_attn_f_conv_b': _L1_attn_in['f_conv_b'], 'L1_attn_f_xproj_w': _L1_attn_in['f_xproj_w'], 'L1_attn_f_dt_w': _L1_attn_in['f_dt_w'], 'L1_attn_f_dt_b': _L1_attn_in['f_dt_b'], 'L1_attn_f_Alog': _L1_attn_in['f_Alog'], 'L1_attn_f_D': _L1_attn_in['f_D'], 'L1_attn_f_out_w': _L1_attn_in['f_out_w'], 'L1_attn_b_in_w': _L1_attn_in['b_in_w'], 'L1_attn_b_conv_w': _L1_attn_in['b_conv_w'], 'L1_attn_b_conv_b': _L1_attn_in['b_conv_b'], 'L1_attn_b_xproj_w': _L1_attn_in['b_xproj_w'], 'L1_attn_b_dt_w': _L1_attn_in['b_dt_w'], 'L1_attn_b_dt_b': _L1_attn_in['b_dt_b'], 'L1_attn_b_Alog': _L1_attn_in['b_Alog'], 'L1_attn_b_D': _L1_attn_in['b_D'], 'L1_attn_b_out_w': _L1_attn_in['b_out_w'], 'L1_ffn_gate_w': _L1_ffn_in['gate_w'], 'L1_ffn_gate_b': _L1_ffn_in['gate_b'], 'L1_ffn_w1': _L1_ffn_in['w1'], 'L1_ffn_b1': _L1_ffn_in['b1'], 'L1_ffn_w3': _L1_ffn_in['w3'], 'L1_ffn_b3': _L1_ffn_in['b3'], 'L1_ffn_w2': _L1_ffn_in['w2'], 'L1_ffn_b2': _L1_ffn_in['b2'], 'L1_ffn_sw1': _L1_ffn_in['sw1'], 'L1_ffn_sb1': _L1_ffn_in['sb1'], 'L1_ffn_sw3': _L1_ffn_in['sw3'], 'L1_ffn_sb3': _L1_ffn_in['sb3'], 'L1_ffn_sw2': _L1_ffn_in['sw2'], 'L1_ffn_sb2': _L1_ffn_in['sb2'], 'L2_xattn_Wq': _L2_xattn_in['Wq'], 'L2_xattn_Wk': _L2_xattn_in['Wk'], 'L2_xattn_Wv': _L2_xattn_in['Wv'], 'L2_attn_in_proj_w': _L2_attn_in['in_proj_w'], 'L2_attn_conv_w': _L2_attn_in['conv_w'], 'L2_attn_conv_b': _L2_attn_in['conv_b'], 'L2_attn_x_proj_w': _L2_attn_in['x_proj_w'], 'L2_attn_A_log': _L2_attn_in['A_log'], 'L2_attn_D_param': _L2_attn_in['D_param'], 'L2_attn_out_proj_w': _L2_attn_in['out_proj_w'], 'L2_ffn_Wr': _L2_ffn_in['Wr'], 'L2_ffn_br': _L2_ffn_in['br'], 'L2_ffn_W1': _L2_ffn_in['W1'], 'L2_ffn_b1': _L2_ffn_in['b1'], 'L2_ffn_W2': _L2_ffn_in['W2'], 'L2_ffn_b2': _L2_ffn_in['b2'], 'L3_xattn_Wq': _L3_xattn_in['Wq'], 'L3_xattn_bq': _L3_xattn_in['bq'], 'L3_xattn_Wk': _L3_xattn_in['Wk'], 'L3_xattn_bk': _L3_xattn_in['bk'], 'L3_xattn_Wv': _L3_xattn_in['Wv'], 'L3_xattn_bv': _L3_xattn_in['bv'], 'L3_xattn_Wp': _L3_xattn_in['Wp'], 'L3_xattn_bp': _L3_xattn_in['bp'], 'L3_attn_Wq': _L3_attn_in['Wq'], 'L3_attn_Wk': _L3_attn_in['Wk'], 'L3_attn_Wv': _L3_attn_in['Wv'], 'L3_attn_Wo': _L3_attn_in['Wo'], 'L3_ffn_W_qkv': _L3_ffn_in['W_qkv'], 'L3_ffn_b_qkv': _L3_ffn_in['b_qkv'], 'L3_ffn_W_gate': _L3_ffn_in['W_gate'], 'L3_ffn_b_gate': _L3_ffn_in['b_gate'], 'L3_ffn_W_experts': _L3_ffn_in['W_experts'], 'L3_ffn_b_experts': _L3_ffn_in['b_experts']}

def reference(x, ctx_1024, mask_BxS2_bf1, mask_1x1xSxS2_fk1, mask_BxSxS2_ff0, L0_xattn_ln_x_g, L0_xattn_ln_x_b, L0_xattn_ln_l_g, L0_xattn_ln_l_b, L0_xattn_qn_g, L0_xattn_kn_g, L0_xattn_Wq, L0_xattn_Wkv, L0_xattn_Wout, L0_xattn_bout, L0_attn_Wq, L0_attn_bq, L0_attn_Wk, L0_attn_bk, L0_attn_Wv, L0_attn_bv, L0_attn_Wo, L0_attn_bo, L0_ffn_Wr, L0_ffn_br, L0_ffn_W1, L0_ffn_b1, L0_ffn_W2, L0_ffn_b2, L1_xattn_wq, L1_xattn_bq, L1_xattn_wk, L1_xattn_bk, L1_xattn_wv, L1_xattn_bv, L1_xattn_wo, L1_xattn_bo, L1_attn_ln_g, L1_attn_ln_b, L1_attn_f_in_w, L1_attn_f_conv_w, L1_attn_f_conv_b, L1_attn_f_xproj_w, L1_attn_f_dt_w, L1_attn_f_dt_b, L1_attn_f_Alog, L1_attn_f_D, L1_attn_f_out_w, L1_attn_b_in_w, L1_attn_b_conv_w, L1_attn_b_conv_b, L1_attn_b_xproj_w, L1_attn_b_dt_w, L1_attn_b_dt_b, L1_attn_b_Alog, L1_attn_b_D, L1_attn_b_out_w, L1_ffn_gate_w, L1_ffn_gate_b, L1_ffn_w1, L1_ffn_b1, L1_ffn_w3, L1_ffn_b3, L1_ffn_w2, L1_ffn_b2, L1_ffn_sw1, L1_ffn_sb1, L1_ffn_sw3, L1_ffn_sb3, L1_ffn_sw2, L1_ffn_sb2, L2_xattn_Wq, L2_xattn_Wk, L2_xattn_Wv, L2_attn_in_proj_w, L2_attn_conv_w, L2_attn_conv_b, L2_attn_x_proj_w, L2_attn_A_log, L2_attn_D_param, L2_attn_out_proj_w, L2_ffn_Wr, L2_ffn_br, L2_ffn_W1, L2_ffn_b1, L2_ffn_W2, L2_ffn_b2, L3_xattn_Wq, L3_xattn_bq, L3_xattn_Wk, L3_xattn_bk, L3_xattn_Wv, L3_xattn_bv, L3_xattn_Wp, L3_xattn_bp, L3_attn_Wq, L3_attn_Wk, L3_attn_Wv, L3_attn_Wo, L3_ffn_W_qkv, L3_ffn_b_qkv, L3_ffn_W_gate, L3_ffn_b_gate, L3_ffn_W_experts, L3_ffn_b_experts):
    import jax
    import jax.numpy as jnp

    def _L0_xattn_ref(x, latents, mask, ln_x_g, ln_x_b, ln_l_g, ln_l_b, qn_g, kn_g, Wq, Wkv, Wout, bout):
        import jax, jax.numpy as jnp
        import numpy as np
        DIM = 256
        DIM_LATENT = 256
        DIM_HEAD = 64
        HEADS = 16
        INNER = HEADS * DIM_HEAD

        def layernorm(x, g, b, eps=1e-05):
            m = jnp.mean(x, axis=-1, keepdims=True)
            v = jnp.mean((x - m) ** 2, axis=-1, keepdims=True)
            return (x - m) / jnp.sqrt(v + eps) * g + b

        def rmsnorm(x, gamma, eps=1e-08):
            n = jnp.linalg.norm(x, axis=-1, keepdims=True) * x.shape[-1] ** (-0.5)
            return x / jnp.maximum(n, eps) * gamma
        b, n, _ = x.shape
        m = latents.shape[1]
        h, d = (HEADS, DIM_HEAD)
        scale = d ** (-0.5)
        xn = layernorm(x, ln_x_g, ln_x_b)
        ln = layernorm(latents, ln_l_g, ln_l_b)
        q = (ln @ Wq).reshape(b, m, h, d).transpose(0, 2, 1, 3)
        kv = jnp.concatenate([xn @ Wkv, ln @ Wkv], axis=1)
        kv = kv.reshape(b, n + m, 2, h, d)
        k = kv[:, :, 0].transpose(0, 2, 1, 3)
        v = kv[:, :, 1].transpose(0, 2, 1, 3)
        qn = rmsnorm(q, qn_g) * scale
        kn = rmsnorm(k, kn_g)
        sim = jnp.einsum('bhid,bhjd->bhij', qn, kn)
        max_neg = -jnp.finfo(sim.dtype).max
        padded_mask = jnp.concatenate([mask, jnp.ones((b, m), bool)], axis=1)
        sim = jnp.where(padded_mask[:, None, None, :], sim, max_neg)
        attn = jax.nn.softmax(sim.astype(jnp.float32), axis=-1).astype(sim.dtype)
        out = jnp.einsum('bhij,bhjd->bhid', attn, v)
        out = out.transpose(0, 2, 1, 3).reshape(b, m, h * d)
        return out @ Wout + bout

    def _L0_attn_ref(x, Wq, bq, Wk, bk, Wv, bv, Wo, bo):
        import jax, jax.numpy as jnp
        import numpy as np
        D_MODEL = 256
        N_HEADS = 16
        WINDOW = 64
        SEQ = 1024
        BATCH = 1
        NEG_INF = -1e+30
        B, S, D = x.shape
        H = N_HEADS
        hd = D // H
        q = (x @ Wq + bq).reshape(B, S, H, hd).transpose(0, 2, 1, 3)
        k = (x @ Wk + bk).reshape(B, S, H, hd).transpose(0, 2, 1, 3)
        v = (x @ Wv + bv).reshape(B, S, H, hd).transpose(0, 2, 1, 3)
        scale = 1.0 / jnp.sqrt(jnp.asarray(hd, x.dtype))
        scores = jnp.einsum('bhqd,bhkd->bhqk', q, k) * scale
        i = jnp.arange(S)[:, None]
        j = jnp.arange(S)[None, :]
        allowed = (j <= i) & (i - j < WINDOW)
        scores = jnp.where(allowed, scores, NEG_INF)
        attn = jax.nn.softmax(scores, axis=-1)
        out = jnp.einsum('bhqk,bhkd->bhqd', attn, v)
        out = out.transpose(0, 2, 1, 3).reshape(B, S, D)
        return out @ Wo + bo

    def _L0_ffn_ref(inputs, Wr, br, W1, b1, W2, b2):
        import jax, jax.numpy as jnp
        import numpy as np
        B, T, D = inputs.shape
        E = Wr.shape[1]
        x = inputs.reshape(B * T, D)
        N = x.shape[0]
        C = N // E
        logits = x @ Wr + br
        probs = jax.nn.softmax(logits, axis=-1)
        gate = jnp.max(probs, axis=-1, keepdims=True)
        idx = jnp.argmax(probs, axis=-1)
        mask = jax.nn.one_hot(idx, E, dtype=jnp.float32)
        pos = (jnp.cumsum(mask, axis=0) * mask).astype(jnp.int32)
        mask = mask * (pos < C).astype(jnp.float32)
        mask_flat = jnp.sum(mask, axis=-1, keepdims=True)
        gate = gate * mask_flat
        combine = (gate * mask_flat * jax.nn.one_hot(idx, E, dtype=jnp.float32))[..., None] * jax.nn.one_hot(pos, C, dtype=jnp.float32)
        dispatch = combine
        expert_in = jnp.einsum('nd,nec->ecd', x, dispatch)
        h = jax.nn.relu(jnp.einsum('ecd,edf->ecf', expert_in, W1) + b1[:, None, :])
        eo = jnp.einsum('ecf,efd->ecd', h, W2) + b2[:, None, :]
        out = jnp.einsum('ecd,nec->nd', eo, combine)
        return out.reshape(B, T, D)

    def _L1_xattn_ref(q, k, v, mask, wq, bq, wk, bk, wv, bv, wo, bo):
        import jax, jax.numpy as jnp
        import numpy as np
        D_MODEL = 256
        NUM_HEADS = 16
        DEPTH = D_MODEL // NUM_HEADS
        B, S = (4, 512)

        def _split_heads(x):
            b, s, _ = x.shape
            return x.reshape(b, s, NUM_HEADS, DEPTH).transpose(0, 2, 1, 3)
        qh = _split_heads(q @ wq + bq)
        kh = _split_heads(k @ wk + bk)
        vh = _split_heads(v @ wv + bv)
        inv_sqrt_dk = 1.0 / jnp.sqrt(jnp.asarray(DEPTH, jnp.float32))
        logits = jnp.einsum('bhqd,bhkd->bhqk', qh, kh) * inv_sqrt_dk
        logits = logits + mask * -1000000000.0
        attn = jax.nn.softmax(logits, axis=-1)
        out = jnp.einsum('bhqk,bhkd->bhqd', attn, vh)
        out = out.transpose(0, 2, 1, 3).reshape(q.shape[0], -1, D_MODEL)
        return out @ wo + bo

    def _L1_attn_ref(x, ln_g, ln_b, f_in_w, f_conv_w, f_conv_b, f_xproj_w, f_dt_w, f_dt_b, f_Alog, f_D, f_out_w, b_in_w, b_conv_w, b_conv_b, b_xproj_w, b_dt_w, b_dt_b, b_Alog, b_D, b_out_w):
        import jax, jax.numpy as jnp
        import numpy as np

        def _layernorm(x, g, b, eps=1e-05):
            m = x.mean(-1, keepdims=True)
            v = x.var(-1, keepdims=True)
            return (x - m) * jax.lax.rsqrt(v + eps) * g + b

        def _mamba(x, in_w, conv_w, conv_b, xproj_w, dt_w, dt_b, A_log, D, out_w):
            Bsz, L, _ = x.shape
            d_state = A_log.shape[1]
            dt_rank = dt_w.shape[1]
            d_conv = conv_w.shape[1]
            u, z = jnp.split(x @ in_w.T, 2, axis=-1)
            u_pad = jnp.pad(u, ((0, 0), (d_conv - 1, 0), (0, 0)))
            u = sum((u_pad[:, k:k + L, :] * conv_w[:, k] for k in range(d_conv))) + conv_b
            u = jax.nn.silu(u)
            dbc = u @ xproj_w.T
            dt = jax.nn.softplus(dbc[..., :dt_rank] @ dt_w.T + dt_b)
            Bm = dbc[..., dt_rank:dt_rank + d_state]
            Cm = dbc[..., dt_rank + d_state:]
            A = -jnp.exp(A_log)
            dA = jnp.exp(dt[..., None] * A)
            dBu = (dt * u)[..., None] * Bm[:, :, None, :]

            def step(h, inp):
                dA_t, dBu_t, C_t = inp
                h = dA_t * h + dBu_t
                return (h, jnp.einsum('bdn,bn->bd', h, C_t))
            h0 = jnp.zeros((Bsz, u.shape[-1], d_state), x.dtype)
            _, ys = jax.lax.scan(step, h0, (dA.swapaxes(0, 1), dBu.swapaxes(0, 1), Cm.swapaxes(0, 1)))
            y = ys.swapaxes(0, 1) + u * D
            return y * jax.nn.silu(z) @ out_w.T
        res = x
        xn = _layernorm(x, ln_g, ln_b)
        out_f = _mamba(xn, f_in_w, f_conv_w, f_conv_b, f_xproj_w, f_dt_w, f_dt_b, f_Alog, f_D, f_out_w)
        out_b = _mamba(xn[:, ::-1, :], b_in_w, b_conv_w, b_conv_b, b_xproj_w, b_dt_w, b_dt_b, b_Alog, b_D, b_out_w)[:, ::-1, :]
        return res + out_f + out_b

    def _L1_ffn_ref(x, gate_w, gate_b, w1, b1, w3, b3, w2, b2, sw1, sb1, sw3, sb3, sw2, sb2):
        import jax, jax.numpy as jnp
        import numpy as np
        ALPHA = 1.702
        LIMIT = 7.0
        TOPK = 2
        D, I, E = (256, 512, 8)
        B, S = (2, 512)

        def swiglu(x):
            g = x[..., ::2]
            l = x[..., 1::2]
            g = jnp.minimum(g, LIMIT)
            l = jnp.clip(l, -LIMIT, LIMIT)
            return g * jax.nn.sigmoid(ALPHA * g) * (l + 1.0)
        b, s, d = x.shape
        xt = x.reshape(-1, d)
        scores = jax.nn.softmax(xt @ gate_w.T, axis=-1)
        biased = scores + gate_b
        _, idx = jax.lax.top_k(biased, TOPK)
        weights = jnp.take_along_axis(scores, idx, axis=-1)
        comb = (weights[..., None] * jax.nn.one_hot(idx, E, dtype=xt.dtype)).sum(1)

        def body(acc, p):
            ew1, eb1, ew3, eb3, ew2, eb2, ce = p
            h = swiglu((xt @ ew1 + eb1) * (xt @ ew3 + eb3))
            return (acc + ce[:, None] * (h @ ew2 + eb2), None)
        routed, _ = jax.lax.scan(body, jnp.zeros_like(xt), (w1, b1, w3, b3, w2, b2, comb.T))
        shared = swiglu((xt @ sw1 + sb1) * (xt @ sw3 + sb3)) @ sw2 + sb2
        return (routed + shared).reshape(b, s, d)

    def _L2_xattn_ref(x1, x2, x3, mask, Wq, Wk, Wv):
        import jax, jax.numpy as jnp
        import numpy as np
        B, S, D, H = (4, 512, 256, 256)
        q = jnp.einsum('bsd,hd->bsh', x1, Wq)
        k = jnp.einsum('bsd,hd->bsh', x2, Wk)
        v = jnp.einsum('bsd,hd->bsh', x3, Wv)
        scale = 1.0 / jnp.sqrt(jnp.float32(H))
        scores = jnp.einsum('bqh,bkh->bqk', q, k) * scale
        weights = jax.nn.softmax(scores + mask, axis=-1)
        out = jnp.einsum('bqk,bkh->bqh', weights, v)
        return out

    def _L2_attn_ref(x, in_proj_w, conv_w, conv_b, x_proj_w, A_log, D_param, out_proj_w):
        import jax, jax.numpy as jnp
        import numpy as np
        BATCH, SEQ, D_MODEL = (4, 512, 256)
        D_STATE, D_CONV = (16, 4)

        def _silu(u):
            return u * jax.nn.sigmoid(u)
        seq_len = x.shape[1]
        d_state = A_log.shape[1]
        xz = jnp.einsum('bld,ed->ble', x, in_proj_w)
        x_ssm, z = jnp.split(xz, 2, axis=-1)
        xpad = jnp.pad(x_ssm, ((0, 0), (D_CONV - 1, 0), (0, 0)))
        x_conv = conv_b
        acc = jnp.zeros_like(x_ssm)
        for k in range(D_CONV):
            acc = acc + xpad[:, k:k + seq_len, :] * conv_w[:, k]
        x_conv = _silu(acc + conv_b)
        ssm_params = jnp.einsum('bld,ed->ble', x_conv, x_proj_w)
        Bm = ssm_params[..., :d_state]
        Cm = ssm_params[..., d_state:2 * d_state]
        delta = jax.nn.softplus(ssm_params[..., -1:])
        A = -jnp.exp(A_log)

        def step(h, inp):
            xt, Bt, Ct, dt = inp
            dA = jnp.exp(dt[:, :, None] * A[None])
            h = dA * h + dt[:, :, None] * Bt[:, None, :] * xt[:, :, None]
            y = jnp.einsum('bdn,bn->bd', h, Ct)
            return (h, y)
        h0 = jnp.zeros((x.shape[0], x.shape[2], d_state), x.dtype)
        xs = (jnp.swapaxes(x_conv, 0, 1), jnp.swapaxes(Bm, 0, 1), jnp.swapaxes(Cm, 0, 1), jnp.swapaxes(delta, 0, 1))
        _, ys = jax.lax.scan(step, h0, xs)
        y = jnp.swapaxes(ys, 0, 1)
        y = y + D_param * x_conv
        y = y * _silu(z)
        return jnp.einsum('bld,ed->ble', y, out_proj_w)

    def _L2_ffn_ref(x, Wr, br, W1, b1, W2, b2):
        import jax, jax.numpy as jnp
        import numpy as np
        K = 2
        E = Wr.shape[-1]
        scores = jnp.einsum('bsd,de->bse', x, Wr) + br
        _, topk_idx = jax.lax.top_k(scores, K)
        indicator = jax.nn.one_hot(topk_idx, E, dtype=scores.dtype).sum(-2)
        neg_inf = jnp.asarray(-jnp.inf, scores.dtype)
        weights = jax.nn.softmax(jnp.where(indicator > 0, scores, neg_inf), axis=-1)
        out = jnp.zeros_like(x)
        for i in range(E):
            xi = x * indicator[..., i:i + 1]
            h = jax.nn.relu(jnp.einsum('bsd,dh->bsh', xi, W1[i]) + b1[i])
            yi = jnp.einsum('bsh,hd->bsd', h, W2[i]) + b2[i]
            out = out + yi * weights[..., i:i + 1]
        return out

    def _L3_xattn_ref(x, y, Wq, bq, Wk, bk, Wv, bv, Wp, bp):
        import jax, jax.numpy as jnp
        import numpy as np
        B, T, C, H = (4, 1024, 256, 16)
        D = C // H

        def _heads(t):
            b, n, c = t.shape
            return t.reshape(b, n, H, D).transpose(0, 2, 1, 3)
        q = jax.nn.softmax(_heads(x @ Wq.T + bq), axis=-1)
        k = jax.nn.softmax(_heads(y @ Wk.T + bk), axis=-1)
        v = _heads(y @ Wv.T + bv)
        k_cumsum = jnp.sum(k, axis=-2, keepdims=True)
        D_inv = 1.0 / jnp.sum(q * k_cumsum, axis=-1, keepdims=True)
        kv = jnp.einsum('bhnd,bhne->bhde', k, v)
        out = q + jnp.einsum('bhnd,bhde->bhne', q, kv) * D_inv
        out = out.transpose(0, 2, 1, 3).reshape(x.shape[0], x.shape[1], C)
        return out @ Wp.T + bp

    def _L3_attn_ref(x, Wq, Wk, Wv, Wo):
        import jax, jax.numpy as jnp
        import numpy as np
        import math
        B, S, D = (4, 512, 256)
        H, KV = (16, 4)
        HD = D // H
        GROUPS = H // KV

        def _alibi_slopes(n):
            start = 2.0 ** (-2.0 ** (-(math.log2(n) - 3)))
            return np.array([start * start ** i for i in range(n)], dtype=np.float32)
        b, s, _ = x.shape
        scale = HD ** (-0.5)
        q = (x @ Wq).reshape(b, s, H, HD).transpose(0, 2, 1, 3)
        k = (x @ Wk).reshape(b, s, KV, HD).transpose(0, 2, 1, 3)
        v = (x @ Wv).reshape(b, s, KV, HD).transpose(0, 2, 1, 3)
        k = jnp.repeat(k, GROUPS, axis=1)
        v = jnp.repeat(v, GROUPS, axis=1)
        attn = jnp.einsum('bhqd,bhkd->bhqk', q, k) * scale
        slopes = jnp.asarray(_alibi_slopes(H))
        pos = jnp.arange(s, dtype=jnp.float32)
        rel = pos[None, :] - pos[:, None]
        attn = attn + slopes[None, :, None, None] * rel[None, None, :, :]
        attn = jax.nn.softmax(attn, axis=-1)
        out = jnp.einsum('bhqk,bhkd->bhqd', attn, v)
        out = out.transpose(0, 2, 1, 3).reshape(b, s, H * HD)
        return out @ Wo

    def _L3_ffn_ref(x, W_qkv, b_qkv, W_gate, b_gate, W_experts, b_experts):
        import jax, jax.numpy as jnp
        import numpy as np
        NUM_HEADS = 16
        TOP_K = 2
        B, S, D = x.shape
        H = NUM_HEADS
        hd = D // H
        E = W_gate.shape[-1]
        qkv = (x @ W_qkv + b_qkv).reshape(B, S, 3, H, hd)
        q, k, v = (qkv[:, :, 0], qkv[:, :, 1], qkv[:, :, 2])
        attn = jnp.einsum('bqhd,bkhd->bhqk', q, k) / jnp.sqrt(jnp.asarray(hd, x.dtype))
        attn = jax.nn.softmax(attn, axis=-1)
        attn_out = jnp.einsum('bhqk,bkhd->bqhd', attn, v).reshape(B, S, D)
        gate = jax.nn.softmax(x @ W_gate + b_gate, axis=-1)
        top_g, top_i = jax.lax.top_k(gate, TOP_K)
        combine = jnp.sum(jax.nn.one_hot(top_i, E, dtype=x.dtype) * top_g[..., None], axis=2)
        expert_out = jnp.einsum('bsd,edf->bsef', x, W_experts) + b_experts
        moe_out = jnp.einsum('bsef,bse->bsf', expert_out, combine)
        return attn_out + moe_out
    x = x + _L0_xattn_ref(ctx_1024, _layernorm(x, axis=-1), mask_BxS2_bf1, L0_xattn_ln_x_g, L0_xattn_ln_x_b, L0_xattn_ln_l_g, L0_xattn_ln_l_b, L0_xattn_qn_g, L0_xattn_kn_g, L0_xattn_Wq, L0_xattn_Wkv, L0_xattn_Wout, L0_xattn_bout)
    x = x + _L0_attn_ref(_layernorm(x, axis=-1), L0_attn_Wq, L0_attn_bq, L0_attn_Wk, L0_attn_bk, L0_attn_Wv, L0_attn_bv, L0_attn_Wo, L0_attn_bo)
    x = x + _L0_ffn_ref(_layernorm(x, axis=-1), L0_ffn_Wr, L0_ffn_br, L0_ffn_W1, L0_ffn_b1, L0_ffn_W2, L0_ffn_b2)
    x = x + _L1_xattn_ref(_layernorm(x, axis=-1), ctx_1024, ctx_1024, mask_1x1xSxS2_fk1, L1_xattn_wq, L1_xattn_bq, L1_xattn_wk, L1_xattn_bk, L1_xattn_wv, L1_xattn_bv, L1_xattn_wo, L1_xattn_bo)
    x = x + _L1_attn_ref(_layernorm(x, axis=-1), L1_attn_ln_g, L1_attn_ln_b, L1_attn_f_in_w, L1_attn_f_conv_w, L1_attn_f_conv_b, L1_attn_f_xproj_w, L1_attn_f_dt_w, L1_attn_f_dt_b, L1_attn_f_Alog, L1_attn_f_D, L1_attn_f_out_w, L1_attn_b_in_w, L1_attn_b_conv_w, L1_attn_b_conv_b, L1_attn_b_xproj_w, L1_attn_b_dt_w, L1_attn_b_dt_b, L1_attn_b_Alog, L1_attn_b_D, L1_attn_b_out_w)
    x = x + _L1_ffn_ref(_layernorm(x, axis=-1), L1_ffn_gate_w, L1_ffn_gate_b, L1_ffn_w1, L1_ffn_b1, L1_ffn_w3, L1_ffn_b3, L1_ffn_w2, L1_ffn_b2, L1_ffn_sw1, L1_ffn_sb1, L1_ffn_sw3, L1_ffn_sb3, L1_ffn_sw2, L1_ffn_sb2)
    x = x + _L2_xattn_ref(_layernorm(x, axis=-1), ctx_1024, ctx_1024, mask_BxSxS2_ff0, L2_xattn_Wq, L2_xattn_Wk, L2_xattn_Wv)
    x = x + _L2_attn_ref(_layernorm(x, axis=-1), L2_attn_in_proj_w, L2_attn_conv_w, L2_attn_conv_b, L2_attn_x_proj_w, L2_attn_A_log, L2_attn_D_param, L2_attn_out_proj_w)
    x = x + _L2_ffn_ref(_layernorm(x, axis=-1), L2_ffn_Wr, L2_ffn_br, L2_ffn_W1, L2_ffn_b1, L2_ffn_W2, L2_ffn_b2)
    x = x + _L3_xattn_ref(_layernorm(x, axis=-1), ctx_1024, L3_xattn_Wq, L3_xattn_bq, L3_xattn_Wk, L3_xattn_bk, L3_xattn_Wv, L3_xattn_bv, L3_xattn_Wp, L3_xattn_bp)
    x = x + _L3_attn_ref(_layernorm(x, axis=-1), L3_attn_Wq, L3_attn_Wk, L3_attn_Wv, L3_attn_Wo)
    x = x + _L3_ffn_ref(_layernorm(x, axis=-1), L3_ffn_W_qkv, L3_ffn_b_qkv, L3_ffn_W_gate, L3_ffn_b_gate, L3_ffn_W_experts, L3_ffn_b_experts)
    return x

_drawn_inputs = setup_inputs


def setup_inputs(seed=0):
    import zlib

    import numpy as np

    out = dict(_drawn_inputs(seed))
    spreads = {'L0_xattn_ln_x_g': (1.0, 0.2),
     'L0_xattn_ln_x_b': (0.0, 0.1),
     'L0_xattn_ln_l_g': (1.0, 0.2),
     'L0_xattn_ln_l_b': (0.0, 0.1),
     'L0_xattn_qn_g': (1.0, 0.2),
     'L0_xattn_kn_g': (1.0, 0.2),
     'L0_xattn_bout': (0.0, 0.1),
     'L0_attn_bq': (0.0, 0.1),
     'L0_attn_bk': (0.0, 0.1),
     'L0_attn_bv': (0.0, 0.1),
     'L0_attn_bo': (0.0, 0.1),
     'L0_ffn_br': (0.0, 0.1),
     'L0_ffn_b1': (0.0, 0.1),
     'L0_ffn_b2': (0.0, 0.1),
     'L1_xattn_bq': (0.0, 0.1),
     'L1_xattn_bk': (0.0, 0.1),
     'L1_xattn_bv': (0.0, 0.1),
     'L1_xattn_bo': (0.0, 0.1),
     'L1_attn_ln_g': (1.0, 0.2),
     'L1_attn_ln_b': (0.0, 0.1),
     'L1_attn_f_conv_b': (0.0, 0.1),
     'L1_attn_f_D': (1.0, 0.2),
     'L1_attn_b_conv_b': (0.0, 0.1),
     'L1_attn_b_D': (1.0, 0.2),
     'L2_attn_D_param': (1.0, 0.2),
     'L3_xattn_bq': (0.0, 0.1),
     'L3_xattn_bk': (0.0, 0.1),
     'L3_xattn_bv': (0.0, 0.1),
     'L3_xattn_bp': (0.0, 0.1),
     'L3_ffn_b_qkv': (0.0, 0.1),
     'L3_ffn_b_gate': (0.0, 0.1),
     'L3_ffn_b_experts': (0.0, 0.1)}
    factors = {}
    for name, (base, spread) in spreads.items():
        noise = np.random.default_rng([zlib.crc32(name.encode()), seed]).standard_normal(out[name].shape)
        drawn = base * np.exp(spread * noise) if base else spread * noise
        out[name] = jnp.asarray(drawn.astype(out[name].dtype))
    for name, factor in factors.items():
        out[name] = (out[name] * factor).astype(out[name].dtype)
    return out
```

```python
from contextlib import ExitStack, contextmanager

import numpy as np

import concourse.bass as bass
from concourse import mybir

P = 128
B, S, D = 8, 64, 256
N = B * S
NT = N // P
KT = D // P
CTX = 1601
CT = -(-CTX // P)
CLAST = CTX - (CT - 1) * P
H, HD = 16, 16
NP_ = H // 2
EPS = 1e-5

F32 = mybir.dt.float32
U32 = mybir.dt.uint32
ALU = mybir.AluOpType
ACT = mybir.ActivationFunctionType
AX = mybir.AxisListType


def _rows(w):
    k, n = w.shape
    return np.ascontiguousarray(w.reshape(k // P, P, n).transpose(1, 0, 2).reshape(P, -1))


def _col(v):
    return np.ascontiguousarray(v.reshape(-1, P).T)


def _bc(v):
    return np.broadcast_to(v.reshape(1, -1), (P, v.size))


def _pad(a):
    out = np.zeros((P,) + a.shape[1:], a.dtype)
    out[:a.shape[0]] = a
    return out


class Chain:

    def __init__(self, eng, sem):
        self.eng, self.sem, self.n, self.i = eng, sem, 0, None

    def value(self):
        return self.n if self.i is None else self.i * self.per + self.n

    def __call__(self, ins):
        ins.then_inc(self.sem, 1)
        self.n += 1
        self.eng.wait_ge(self.sem, self.value())
        return ins

    @contextmanager
    def loop(self, i, trips, per):
        base = self.n
        self.i, self.per = i, per
        yield
        assert self.n - base == per, (self.n - base)
        self.i = None
        self.n = base + trips * per


def turn(nc, out, tile, ident, carries_wait):
    if carries_wait:
        return nc.tensor.matmul(out, tile, ident, start=True, stop=True)
    return nc.tensor.transpose(out, tile, ident)


def take_wait(L, n=0):
    L.nc.vector.memset(L.unused[:, n:n + 1], 0.0)


class Layer:

    def __init__(self, nc, ctx, aps):
        self.nc, self.aps = nc, aps

        def sb(name, shape, dt=F32):
            return ctx.enter_context(nc.sbuf_tensor(name, shape, dt))

        self.x = sb("x_tok", [P, NT, D])
        self.z = sb("z_tok", [P, NT, D])
        self.zT = sb("z_feat", [P, KT, N])
        self.stats = sb("ln_stats", [P, NT, 6])
        self.mv = sb("ln_mean_var", [P, NT, 2])
        self.rstd = sb("ln_rstd", [P, NT])
        self.unused = sb("unused", [P, 4])
        self.const = sb("const", [P, CONST_COLS])
        self.weights = [sb("weights_a", [P, WCOLS[0]]), sb("weights_b", [P, WCOLS[1]])]
        self.ident = self.const[:, C_IDENT:C_IDENT + P]
        self.flip = self.const[:, C_FLIP:C_FLIP + P]
        self.fold = self.const[:, C_FOLD:C_FOLD + S]
        self.heads8 = self.const[:, C_HEADS:C_HEADS + 8]
        self.pairblk = self.const[:, C_PAIR:C_PAIR + 32]
        self.half = self.const[:, C_HALF:C_HALF + 2]


C_IDENT, C_FLIP, C_FOLD, C_HEADS, C_PAIR, C_HALF, C_CAUSAL, C_IOTA = 0, 128, 256, 320, 328, 360, 362, 426
C_NONHEAD, C_BLK64, C_BLK16 = 434, 434, 562
C_ALIBI = 690
CONST_COLS = 690 + NP_ * S
WCOLS = (9476, 3072)


def constants():
    c = np.zeros((P, CONST_COLS), np.float32)
    r = np.arange(P)
    c[:, C_IDENT:C_IDENT + P] = np.eye(P)
    c[r, C_FLIP + (r // S) * S + (S - 1 - r % S)] = 1
    c[r, C_FOLD + r % S] = 1
    c[r, C_HEADS + r // HD] = 1
    for h in range(2):
        c[h * S:(h + 1) * S, C_PAIR + h * HD:C_PAIR + (h + 1) * HD] = 1
    c[r, C_HALF + r // 64] = 1
    q = r % S
    j = np.arange(S)
    c[:, C_CAUSAL:C_CAUSAL + S] = np.where(j[None, :] <= q[:, None], 0.0, -1e30)
    c[:, C_IOTA:C_IOTA + 8] = np.arange(8)
    c[:, C_BLK64:C_BLK64 + P] = (r[:, None] // 64 == r[None, :] // 64) / 64.0
    c[:, C_BLK16:C_BLK16 + P] = r[:, None] // HD == r[None, :] // HD
    start = 2.0 ** (-2.0 ** (-(np.log2(H) - 3)))
    slopes = np.array([start * start ** i for i in range(H)], dtype=np.float32)
    for p in range(NP_):
        for h in range(2):
            rows = slice(h * S, (h + 1) * S)
            rel = (j[None, :] - j[:, None]).astype(np.float32)
            c[rows, C_ALIBI + p * S:C_ALIBI + (p + 1) * S] = slopes[2 * p + h] * rel
    return c


def psum4(nc, ctx, name):
    def pb(n, shape):
        return ctx.enter_context(nc.psum_tensor(name + n, shape, F32))
    return pb("wide", [P, 4, 512]), pb("bank4", [P, 512]), pb("bank5", [P, 512]), pb("bank67", [P, 2, 512])


def norm_vector(L, dve, chain, ln_stats_ready, rstd_ready, z_ready, x=None, z=None, nx=0):
    nc = L.nc
    x, z = x or L.x, z or L.z
    for t in range(NT):
        last = nc.vector.bn_stats(L.stats[:, t, :], x[:, t, :])
    chain(last)
    for t in range(NT):
        last = nc.vector.bn_aggr(L.mv[:, t, :], L.stats[:, t, :])
    chain(last)
    nc.vector.tensor_scalar(L.rstd[:, :], L.mv[:, :, 1], EPS, None, ALU.add).then_inc(ln_stats_ready, 1)
    dve.wait_ge(rstd_ready, 2 * (nx + 1))
    for t in range(NT):
        last = nc.vector.tensor_scalar(z[:, t, :], x[:, t, :], L.mv[:, t, 0:1], L.rstd[:, t:t + 1],
                                       ALU.subtract, ALU.mult)
    last.then_inc(z_ready, 1)


def norm_scalar(L, act, ln_stats_ready, rstd_ready, nx=0):
    nc = L.nc
    act.wait_ge(ln_stats_ready, nx + 1)
    nc.scalar.activation(L.rstd[:, :], L.rstd[:, :], ACT.Ln).then_inc(rstd_ready, 1)
    act.wait_ge(rstd_ready, 2 * nx + 1)
    nc.scalar.activation(L.rstd[:, :], L.rstd[:, :], ACT.Exp, scale=-0.5).then_inc(rstd_ready, 1)


def turn_tensor(L, wide, z=None, flip=False):
    nc = L.nc
    z = z or L.z
    for k in range(KT):
        for t in range(NT):
            out = wide[:, k, t * P:(t + 1) * P]
            tile = z[:, t, k * P:(k + 1) * P]
            if flip:
                last = nc.tensor.matmul(out, tile, L.flip, start=True, stop=True)
            else:
                last = nc.tensor.transpose(out, tile, L.ident)
    return last


def self_attention(L, nc, name, w, off, scale, bias_cols, mask_bank, x_bias, w_ready, moe=None):
    with ExitStack() as ctx:
        def sb(n, shape, dt=F32):
            return ctx.enter_context(nc.sbuf_tensor(name + n, shape, dt))

        def sem(n):
            s = ctx.enter_context(nc.semaphore(name + n))
            sems.append(s)
            return s
        sems = []
        wide, bS, bO, bT = psum4(nc, ctx, name)
        wq, wk, wv, wo = (w[:, o:o + KT * D].rearrange("p (k n) -> p k n", k=KT) for o in off)
        qT = sb("qT", [P, KT, N])
        kT = sb("kT", [P, KT, N])
        V = sb("V", [S, B, D])
        qd = sb("q_by_head", [P, 2, KT, 8, S])
        hs = sb("head_scale", [P, 8])
        sc = sb("scores", [P, NP_, S])
        pr = sb("probs", [P, NP_, S])
        prT = sb("probsT", [S, NP_, P])
        mx = sb("max", [P, NP_])
        sm = sb("sum", [P, NP_])
        om = sb("out_by_head", [P, NP_, 32])
        aT = sb("attT", [P, KT, N])

        dve_chain = sem("dve_chain")
        ln_stats_ready = sem("ln_stats_ready")
        rstd_ready = sem("rstd_ready")
        z_ready = sem("z_ready")
        zT_turned = sem("zT_turned")
        zT_ready = sem("zT_ready")
        qk_projected = sem("qk_projected")
        qk_ready = sem("qk_ready")
        v_projected = sem("v_projected")
        v_ready = sem("v_ready")
        qd_ready = sem("qd_ready")
        scored = sem("scored")
        shifted = sem("shifted")
        exp_ready = sem("exp_ready")
        probs_turned = sem("probs_turned")
        probsT_ready = sem("probsT_ready")
        pv_done = sem("pv_done")
        om_ready = sem("om_ready")
        merged = sem("merged")
        att_ready = sem("att_ready")
        projected = sem("projected")
        with nc.Block() as block:
            @block.vector
            def _(dve):
                chain = Chain(dve, dve_chain)
                norm_vector(L, dve, chain, ln_stats_ready, rstd_ready, z_ready)
                dve.wait_ge(zT_turned, 1)
                nc.vector.tensor_copy(L.zT[:, 1, :], wide[:, 1, :]).then_inc(zT_ready, 1)
                chain(nc.vector.tensor_scalar(hs[:, :], L.heads8, scale, None, ALU.mult))
                dve.wait_ge(v_projected, 1)
                vps = wide[0:S, :, :].rearrange("p a (b n) -> p (a b) n", n=D)
                if bias_cols:
                    bv = w[0:S, bias_cols[2]:bias_cols[2] + D]
                    nc.vector.tensor_tensor(V[:, :, :], vps, bv.unsqueeze(1).broadcast_to([S, B, D]),
                                            ALU.add).then_inc(v_ready, 1)
                else:
                    nc.vector.tensor_copy(V[:, :, :], vps).then_inc(v_ready, 1)
                dve.wait_ge(qk_ready, 4)
                with dve.Fori(0, B) as b:
                    with chain.loop(b, B, 5):
                        for k in range(KT):
                            last = nc.vector.tensor_tensor(
                                qd[:, 0, k, :, :],
                                qT[:, k, bass.ds(b * S, S)].unsqueeze(1).broadcast_to([P, 8, S]),
                                hs[:, :].unsqueeze(2).broadcast_to([P, 8, S]), ALU.mult)
                        last.then_inc(qd_ready, 1)
                        dve.wait_ge(scored, b + 1)
                        chain(nc.vector.tensor_tensor(sc[:, :, :], bS[:, :].rearrange("p (a s) -> p a s", s=S),
                                                      mask_bank, ALU.add))
                        chain(nc.vector.tensor_reduce(mx[:, :], sc[:, :, :], AX.X, ALU.max))
                        nc.vector.tensor_tensor(sc[:, :, :], sc[:, :, :],
                                                mx[:, :].unsqueeze(2).broadcast_to([P, NP_, S]),
                                                ALU.subtract).then_inc(shifted, 1)
                        dve.wait_ge(exp_ready, b + 1)
                        chain(nc.vector.tensor_reduce(sm[:, :], pr[:, :, :], AX.X, ALU.add))
                        chain(nc.vector.reciprocal(sm[:, :], sm[:, :]))
                        dve.wait_ge(pv_done, b + 1)
                        chain(nc.vector.tensor_tensor(om[:, :, :],
                                                      bO[:, 0:NP_ * 32].rearrange("p (a s) -> p a s", s=32),
                                                      sm[:, :].unsqueeze(2).broadcast_to([P, NP_, 32]), ALU.mult))
                        nc.vector.tensor_tensor(om[:, :, :], om[:, :, :],
                                                L.pairblk.unsqueeze(1).broadcast_to([P, NP_, 32]),
                                                ALU.mult).then_inc(om_ready, 1)
                        dve.wait_ge(merged, b + 1)
                        nc.vector.tensor_copy(aT[:, :, bass.ds(b * S, S)],
                                              bO[:, 256:256 + KT * S].rearrange("p (a s) -> p a s", s=S)
                                              ).then_inc(att_ready, 1)
                dve.wait_ge(projected, 1)
                ps = wide[:, 0:2, :].rearrange("p a (b n) -> p (a b) n", n=D)
                chain(nc.vector.tensor_tensor(L.x[:, :, :], L.x[:, :, :], ps, ALU.add))
                if bias_cols and bias_cols[3] is not None:
                    bo = w[:, bias_cols[3]:bias_cols[3] + D]
                    chain(nc.vector.tensor_tensor(L.x[:, :, :], L.x[:, :, :],
                                                  bo.unsqueeze(1).broadcast_to([P, NT, D]), ALU.add))

            @block.scalar
            def _(act):
                norm_scalar(L, act, ln_stats_ready, rstd_ready)
                act.wait_ge(zT_turned, 1)
                nc.scalar.activation(L.zT[:, 0, :], wide[:, 0, :], ACT.Copy).then_inc(zT_ready, 1)
                act.wait_ge(w_ready[0], w_ready[1])
                for n, dst in enumerate((qT, kT)):
                    for m in range(KT):
                        act.wait_ge(qk_projected, 2 * n + m + 1)
                        src = wide[:, 2 + m, :] if n == 0 else (bS, bO)[m][:, :]
                        if bias_cols:
                            c = bias_cols[n] + m
                            nc.scalar.activation(dst[:, m, :], src, ACT.Identity,
                                                 bias=w[:, c:c + 1]).then_inc(qk_ready, 1)
                        else:
                            nc.scalar.activation(dst[:, m, :], src, ACT.Copy).then_inc(qk_ready, 1)
                with act.Fori(0, B) as b:
                    act.wait_ge(shifted, b + 1)
                    nc.scalar.activation(pr[:, :, :], sc[:, :, :], ACT.Exp).then_inc(exp_ready, 1)
                    act.wait_ge(probs_turned, b + 1)
                    nc.scalar.activation(prT[:, :, :].rearrange("p a s -> p (a s)"),
                                         bT[0:S, :, :].rearrange("p a s -> p (a s)"),
                                         ACT.Copy).then_inc(probsT_ready, 1)

            @block.tensor
            def _(pe):
                pe.wait_ge(z_ready, 1)
                turn_tensor(L, wide).then_inc(zT_turned, 1)
                pe.wait_ge(w_ready[0], w_ready[1])
                pe.wait_ge(zT_ready, 2)
                for n, wt in enumerate((wq, wk)):
                    for m in range(KT):
                        out = wide[:, 2 + m, :] if n == 0 else (bS, bO)[m][:, :]
                        for k in range(KT):
                            last = nc.tensor.matmul(out, wt[:, k, m * P:(m + 1) * P], L.zT[:, k, :],
                                                    start=(k == 0), stop=(k == KT - 1))
                        last.then_inc(qk_projected, 1)
                pe.wait_ge(qk_ready, 2)
                for b in range(B):
                    out = wide[0:S, b // 2, (b % 2) * D:(b % 2 + 1) * D]
                    for k in range(KT):
                        last = nc.tensor.matmul(out, L.zT[:, k, b * S:(b + 1) * S], wv[:, k, :],
                                                start=(k == 0), stop=(k == KT - 1))
                last.then_inc(v_projected, 1)
                pe.wait_ge(qk_ready, 4)
                pe.wait_ge(v_ready, 1)
                with pe.Fori(0, B) as b:
                    pe.wait_ge(qd_ready, b + 1)
                    for p in range(NP_):
                        k, j = p // 4, p % 4
                        last = nc.tensor.matmul(bS[:, p * S:(p + 1) * S], qd[:, 0, k, 2 * j:2 * j + 2, :],
                                                kT[:, k, bass.ds(b * S, S)], start=True, stop=True)
                    last.then_inc(scored, 1)
                    pe.wait_ge(exp_ready, b + 1)
                    for p in range(NP_):
                        last = turn(nc, bT[0:S, p // 4, (p % 4) * P:(p % 4 + 1) * P], pr[:, p, :], L.ident,
                                    p == 0)
                    last.then_inc(probs_turned, 1)
                    pe.wait_ge(probsT_ready, b + 1)
                    for p in range(NP_):
                        last = nc.tensor.matmul(bO[:, p * 32:(p + 1) * 32], prT[:, p, :],
                                                V[:, b, 32 * p:32 * p + 32], start=True, stop=True)
                    last.then_inc(pv_done, 1)
                    pe.wait_ge(om_ready, b + 1)
                    for k in range(KT):
                        last = nc.tensor.matmul(bO[:, 256 + k * S:256 + (k + 1) * S],
                                                om[:, 4 * k:4 * k + 4, :].rearrange("p a s -> p (a s)"),
                                                L.fold, start=True, stop=True)
                    last.then_inc(merged, 1)
                    pe.wait_ge(att_ready, b + 1)
                for t in range(NT):
                    for k in range(KT):
                        last = nc.tensor.matmul(wide[:, t // 2, (t % 2) * D:(t % 2 + 1) * D],
                                                aT[:, k, t * P:(t + 1) * P], wo[:, k, :],
                                                start=(k == 0), stop=(k == KT - 1))
                last.then_inc(projected, 1)
        end_layer(nc, sems)


def end_layer(nc, sems):
    nums = sorted(s.num if hasattr(s, "num") else s for s in sems)
    nc.all_engine_barrier(sems_to_clear=range(nums[0], nums[-1] + 1))


CHUNKS = [(c, min(512, CTX - c)) for c in range(0, CTX, 512)]


def load_ctx_tok(sp, dst, src, sem):
    full = (CT - 1) * P
    sp.dma_start(dst[:, 0:CT - 1, :], src[0:full, :].rearrange("(t p) d -> p t d", p=P)).then_inc(sem, 16)
    sp.dma_start(dst[0:CLAST, CT - 1, :], src[full:CTX, :]).then_inc(sem, 16)


def tile_rows(t):
    return CLAST if t == CT - 1 else P


def l2_xattn(L, nc, w, w_ready, at):
    name = "L2_xattn_"
    with ExitStack() as ctx:
        sems = []

        def sb(n, shape, dt=F32):
            return ctx.enter_context(nc.sbuf_tensor(name + n, shape, dt))

        def sem(n):
            s = ctx.enter_context(nc.semaphore(name + n))
            sems.append(s)
            return s
        wide, bS, bO, bT = psum4(nc, ctx, name)
        wq, wk, wv = (w[:, at[n]:at[n] + KT * D].rearrange("p (k n) -> p k n", k=KT) for n in ("Wq", "Wk", "Wv"))
        qT = sb("qT", [P, KT, N])
        q2T = sb("q_by_Wk", [P, KT, N])
        qs = sb("q_of_batch", [P, 2, KT, S])
        cT = sb("ctx_feat", [P, 2, KT, CTX])
        ck = sb("ctx_tok", [P, 2, CT, D])
        mk = sb("mask", [S, 2, CTX])
        sc = sb("scores", [S, 2, CTX])
        mx = sb("max", [S, 5])
        nm = sb("neg_max", [S, 1])
        sm = sb("sum", [S, 1])
        rs = sb("rsum", [S, 1])
        pT = sb("probsT", [P, CT, S])
        om = sb("mixed_ctx", [S, D])
        oT = sb("mixed_ctxT", [P, KT, N])
        dve_chain = sem("dve_chain")
        ln_stats_ready = sem("ln_stats_ready")
        rstd_ready = sem("rstd_ready")
        z_ready = sem("z_ready")
        zT_turned = sem("zT_turned")
        zT_ready = sem("zT_ready")
        q_projected = sem("q_projected")
        q_ready = sem("q_ready")
        loaded = [sem("ctx_loaded_0"), sem("ctx_loaded_1")]
        qs_ready = sem("qs_ready")
        scored = sem("scored")
        shifted = sem("shifted")
        exp_ready = sem("exp_ready")
        probs_turned = sem("probs_turned")
        pT_ready = sem("pT_ready")
        mixed = sem("mixed")
        om_ready = sem("om_ready")
        om_turned = sem("om_turned")
        oT_ready = sem("oT_ready")
        projected = sem("projected")
        with nc.Block() as block:
            def load(sp, b, j):
                row = lambda a: a[bass.ds(b, 1)].squeeze(0)
                sp.dma_start(cT[:, j, :, :], row(L.aps["ctx_feat"]).rearrange("(k p) n -> p k n", p=P)
                             ).then_inc(loaded[j], 16)
                load_ctx_tok(sp, ck[:, j, :, :], row(L.aps["ctx_tok"]), loaded[j])
                sp.dma_start(mk[:, j, :], row(L.aps["mask_BSS2"])).then_inc(loaded[j], 16)

            @block.sync
            def _(sp):
                for j in range(2):
                    load(sp, j, j)
                with sp.Fori(0, B // 2 - 1) as i:
                    for j in range(2):
                        sp.wait_ge(mixed, 2 * i + j + 1)
                        load(sp, 2 * i + 2 + j, j)

            @block.vector
            def _(dve):
                chain = Chain(dve, dve_chain)
                norm_vector(L, dve, chain, ln_stats_ready, rstd_ready, z_ready)
                dve.wait_ge(zT_turned, 1)
                nc.vector.tensor_copy(L.zT[:, 1, :], wide[:, 1, :]).then_inc(zT_ready, 1)
                dve.wait_ge(q_ready, 4)
                with dve.Fori(0, B // 2) as i:
                    with chain.loop(i, B // 2, 2 * 3):
                        for j in range(2):
                            b = 2 * i + j
                            nc.vector.tensor_copy(qs[:, j, :, :], q2T[:, :, bass.ds(b * S, S)]).then_inc(qs_ready, 1)
                            dve.wait_ge(loaded[j], 64 * i + 64)
                            dve.wait_ge(scored, b + 1)
                            take_wait(L)
                            for c, (at_c, n) in enumerate(CHUNKS):
                                last = nc.vector.tensor_tensor_reduce(
                                    sc[:, j, at_c:at_c + n], wide[0:S, c, 0:n], mk[:, j, at_c:at_c + n], 1.0,
                                    -3.0e38, ALU.add, ALU.max, mx[:, c:c + 1])
                            chain(last)
                            nc.vector.tensor_reduce(nm[:, :], mx[:, 0:len(CHUNKS)], AX.X, ALU.max, negate=True
                                                    ).then_inc(shifted, 1)
                            dve.wait_ge(exp_ready, b + 1)
                            chain(nc.vector.reciprocal(rs[:, :], sm[:, :]))
                            dve.wait_ge(mixed, b + 1)
                            nc.vector.tensor_scalar(om[:, :], bO[0:S, 0:D], rs[:, 0:1], None, ALU.mult
                                                    ).then_inc(om_ready, 1)
                            dve.wait_ge(om_turned, b + 1)
                            nc.vector.tensor_copy(oT[:, :, bass.ds(b * S, S)],
                                                  bS[:, 0:KT * S].rearrange("p (a s) -> p a s", s=S)
                                                  ).then_inc(oT_ready, 1)
                            chain(nc.vector.memset(rs[:, :], 0.0))
                dve.wait_ge(projected, 1)
                chain(nc.vector.tensor_tensor(L.x[:, :, :], L.x[:, :, :],
                                              wide[:, 0:2, :].rearrange("p a (b n) -> p (a b) n", n=D), ALU.add))

            @block.scalar
            def _(act):
                norm_scalar(L, act, ln_stats_ready, rstd_ready)
                act.wait_ge(zT_turned, 1)
                nc.scalar.activation(L.zT[:, 0, :], wide[:, 0, :], ACT.Copy).then_inc(zT_ready, 1)
                for m in range(KT):
                    act.wait_ge(q_projected, m + 1)
                    nc.scalar.activation(qT[:, m, :], wide[:, 2 + m, :], ACT.Copy).then_inc(q_ready, 1)
                for m in range(KT):
                    act.wait_ge(q_projected, KT + m + 1)
                    nc.scalar.activation(q2T[:, m, :], wide[:, m, :], ACT.Copy, scale=D ** -0.5).then_inc(q_ready, 1)
                with act.Fori(0, B // 2) as i:
                    for j in range(2):
                        b = 2 * i + j
                        act.wait_ge(shifted, b + 1)
                        nc.scalar.activation(sc[:, j, :], sc[:, j, :], ACT.Exp, bias=nm[:, 0:1],
                                             accum_out=sm[:, 0:1]).then_inc(exp_ready, 1)
                        act.wait_ge(probs_turned, b + 1)
                        nc.scalar.activation(pT[:, 0:8, :], bT[:, 0, :].rearrange("p (t s) -> p t s", s=S),
                                             ACT.Copy).then_inc(pT_ready, 1)
                        nc.scalar.activation(pT[:, 8:CT - 1, :],
                                             bT[:, 1, 0:(CT - 9) * S].rearrange("p (t s) -> p t s", s=S),
                                             ACT.Copy).then_inc(pT_ready, 1)
                        nc.scalar.activation(pT[0:CLAST, CT - 1, :], bT[0:CLAST, 1, (CT - 9) * S:(CT - 8) * S],
                                             ACT.Copy).then_inc(pT_ready, 1)

            @block.tensor
            def _(pe):
                pe.wait_ge(z_ready, 1)
                turn_tensor(L, wide).then_inc(zT_turned, 1)
                pe.wait_ge(w_ready[0], w_ready[1])
                pe.wait_ge(zT_ready, 2)
                for n, (wt, src, bank) in enumerate(((wq, L.zT, 2), (wk, qT, 0))):
                    pe.wait_ge(q_ready, 2 * n)
                    for m in range(KT):
                        for k in range(KT):
                            last = nc.tensor.matmul(wide[:, bank + m, :], wt[:, k, m * P:(m + 1) * P],
                                                    src[:, k, :], start=(k == 0), stop=(k == KT - 1))
                        last.then_inc(q_projected, 1)
                pe.wait_ge(q_ready, 4)
                with pe.Fori(0, B // 2) as i:
                    for j in range(2):
                        b = 2 * i + j
                        pe.wait_ge(loaded[j], 64 * i + 64)
                        pe.wait_ge(qs_ready, b + 1)
                        for c, (at_c, n) in enumerate(CHUNKS):
                            for k in range(KT):
                                last = nc.tensor.matmul(wide[0:S, c, 0:n], qs[:, j, k, :],
                                                        cT[:, j, k, at_c:at_c + n], start=(k == 0), stop=(k == KT - 1))
                        last.then_inc(scored, 1)
                        pe.wait_ge(exp_ready, b + 1)
                        for t in range(CT):
                            r = tile_rows(t)
                            last = turn(nc, bT[0:r, t // 8, (t % 8) * S:(t % 8 + 1) * S],
                                        sc[:, j, t * P:t * P + r], L.ident[0:S, 0:S], t == 0)
                        last.then_inc(probs_turned, 1)
                        pe.wait_ge(pT_ready, 3 * b + 3)
                        for t in range(CT):
                            r = tile_rows(t)
                            last = nc.tensor.matmul(bO[0:S, 0:D], pT[0:r, t, :], ck[0:r, j, t, :],
                                                    start=(t == 0), stop=(t == CT - 1))
                        last.then_inc(mixed, 1)
                        pe.wait_ge(om_ready, b + 1)
                        for k in range(KT):
                            last = turn(nc, bS[:, k * S:(k + 1) * S], om[:, k * P:(k + 1) * P],
                                        L.ident[0:S, 0:S], k == 0)
                        last.then_inc(om_turned, 1)
                        pe.wait_ge(oT_ready, b + 1)
                for t in range(NT):
                    for k in range(KT):
                        last = nc.tensor.matmul(wide[:, t // 2, (t % 2) * D:(t % 2 + 1) * D],
                                                oT[:, k, t * P:(t + 1) * P], wv[:, k, :],
                                                start=(k == 0), stop=(k == KT - 1))
                last.then_inc(projected, 1)
        end_layer(nc, sems)


def l0_xattn(L, nc, w, w_ready, at):
    name = "L0_xattn_"
    INNER, DH = 1024, 64
    KC = CTX + S
    TILES = CT + 1
    NQ = INNER // P
    HALVES = [[(0, 512), (512, 512)], [(1024, 512), (1536, KC - 1536)]]
    SPAN = [(0, 1024), (1024, KC - 1024)]
    GROUPS = [(0, 4), (4, 4), (8, 4), (12, 2)]
    with ExitStack() as ctx:
        sems = []

        def sb(n, shape, dt=F32):
            return ctx.enter_context(nc.sbuf_tensor(name + n, shape, dt))

        def sem(n):
            s = ctx.enter_context(nc.semaphore(name + n))
            sems.append(s)
            return s
        wide, bS, bO, bT = psum4(nc, ctx, name)
        wq, wk, wv = (w[:, at[n]:at[n] + KT * INNER].rearrange("p (k n) -> p k n", k=KT) for n in ("Wq", "Wk", "Wv"))
        wo = w[:, at["Wout"]:at["Wout"] + NQ * D].rearrange("p (k n) -> p k n", k=NQ)
        blk = L.const[:, C_BLK64:C_BLK64 + P]
        raw = sb("ctx_raw", [P, CT, D])
        xn = sb("keys_tok", [P, TILES, D])
        xnT = sb("keys_feat", [P, KT, KC])
        ln64 = sb("latents_by_batch", [S, B, D])
        st = sb("ctx_stats", [P, CT, 6])
        mv = sb("ctx_mean_var", [P, CT, 2])
        ve = sb("ctx_rstd", [P, CT])
        mrow = sb("mask_row", [P, KC])
        mrow8 = sb("mask_bytes", [P, CTX], mybir.dt.uint8)
        kn = sb("k_normed", [P, 2, KC])
        sq = sb("k_square", [P, KC])
        sc = sb("scores", [P, KC])
        pT = sb("probsT", [P, TILES, P])
        qT = sb("qT", [P, NQ, N])
        qd = sb("q_by_head", [P, NQ, 2, S])
        gq = sb("q_gain", [P, 1])
        mx = sb("max", [P, 2])
        nm = sb("neg_max", [P, 1])
        sm = sb("sum", [P, 1])
        rs = sb("rsum", [P, 2])
        oh = sb("mixed_tokens", [P, D])
        ohT = sb("mixed_tokensT", [P, KT, P])
        dve_chain = sem("dve_chain")
        ln_stats_ready = sem("ln_stats_ready")
        rstd_ready = sem("rstd_ready")
        z_ready = sem("z_ready")
        zT_turned = sem("zT_turned")
        zT_ready = sem("zT_ready")
        latents_ready = sem("latents_ready")
        latents_moved = sem("latents_moved")
        q_projected = sem("q_projected")
        q_squared = sem("q_squared")
        q_meaned = sem("q_meaned")
        q_clamped = sem("q_clamped")
        q_rnorm = sem("q_rnorm")
        q_ready = sem("q_ready")
        ctx_loaded = sem("ctx_loaded")
        mask_loaded = sem("mask_loaded")
        ctx_var_ready = sem("ctx_var_ready")
        ctx_rstd_ready = sem("ctx_rstd_ready")
        ctx_normed = sem("ctx_normed")
        gained = sem("gained")
        xn_ready = sem("xn_ready")
        mask_ready = sem("mask_ready")
        xn_turned = sem("xn_turned")
        xT_act = sem("xT_act_ready")
        xT_dve = sem("xT_dve_ready")
        qd_ready = sem("qd_ready")
        k_projected = sem("k_projected")
        k_copied = sem("k_copied")
        k_squared = sem("k_squared")
        k_meaned = sem("k_meaned")
        k_clamped = sem("k_clamped")
        k_rnorm = sem("k_rnorm")
        kn_ready = sem("kn_ready")
        scored = sem("scored")
        s_taken = sem("scores_taken")
        shifted = sem("shifted")
        exp_ready = sem("exp_ready")
        sum_inverted = sem("sum_inverted")
        turned = sem("probs_turned")
        pT_even = sem("probsT_even_ready")
        pT_odd = sem("probsT_odd_ready")
        mixed = sem("mixed")
        oh_ready = sem("oh_ready")
        oh_turned = sem("oh_turned")
        ohT_ready = sem("ohT_ready")
        v_applied = sem("v_applied")
        att_ready = sem("att_ready")
        projected = sem("projected")

        def rows(t):
            return {CT - 1: CLAST, CT: S}.get(t, P)

        def start(t):
            return CTX if t == CT else t * P

        def span(h):
            a, n = SPAN[h]
            return wide[:, 2 * h:2 * h + 2, :].rearrange("p a n -> p (a n)")[:, 0:n], a, n
        with nc.Block() as block:
            @block.sync
            def _(sp):
                def load(b):
                    sp.wait_ge(xn_ready, 3 * b)
                    sp.wait_ge(mask_ready, b)
                    load_ctx_tok(sp, raw, L.aps["ctx_tok"][bass.ds(b, 1)].squeeze(0), ctx_loaded)
                    sp.dma_start(mrow8[:, :], L.aps["mask_BS2"][bass.ds(b, 1), :].broadcast_to([P, CTX])
                                 ).then_inc(mask_loaded, 16)
                load(0)
                sp.wait_ge(latents_ready, 1)
                for h in range(2):
                    sp.dma_start(ln64[:, :, :].rearrange("p (t h) d -> p h t d", h=2)[:, h, :, :],
                                 L.z[h * S:(h + 1) * S, :, :]).then_inc(latents_moved, 16)
                with sp.Fori(0, B - 1) as i:
                    load(i + 1)

            def ctx_stats(dve, chain, b):
                dve.wait_ge(ctx_loaded, 32 * b + 32)
                for t in range(CT):
                    r = rows(t)
                    last = nc.vector.bn_stats(st[0:r, t, :], raw[0:r, t, :])
                chain(last)
                take_wait(L, 3)
                for t in range(CT):
                    r = rows(t)
                    last = nc.vector.bn_aggr(mv[0:r, t, :], st[0:r, t, :])
                chain(last)
                nc.vector.tensor_scalar(ve[:, :], mv[:, :, 1], EPS, None, ALU.add).then_inc(ctx_var_ready, 1)

            def ctx_norm(dve, b):
                dve.wait_ge(ctx_rstd_ready, 2 * b + 2)
                for t in range(CT):
                    r = rows(t)
                    last = nc.vector.tensor_scalar(raw[0:r, t, :], raw[0:r, t, :], mv[0:r, t, 0:1], ve[0:r, t:t + 1],
                                                   ALU.subtract, ALU.mult)
                last.then_inc(ctx_normed, 1)

            @block.vector
            def _(dve):
                chain = Chain(dve, dve_chain)
                norm_vector(L, dve, chain, ln_stats_ready, rstd_ready, z_ready)
                dve.wait_ge(z_ready, 1)
                norm_vector(L, dve, chain, ln_stats_ready, rstd_ready, z_ready, x=L.z, nx=1)
                dve.wait_ge(z_ready, 2)
                dve.wait_ge(w_ready[0], w_ready[1])
                g = lambda n: w[:, at[n]:at[n] + D].unsqueeze(1).broadcast_to([P, NT, D])
                chain(nc.vector.tensor_tensor(L.z[:, :, :], L.z[:, :, :], g("ln_l_g"), ALU.mult))
                nc.vector.tensor_tensor(L.z[:, :, :], L.z[:, :, :], g("ln_l_b"), ALU.add).then_inc(latents_ready, 1)
                chain(nc.vector.tensor_scalar(gq[:, :], w[:, at["qn_g"]:at["qn_g"] + 1], DH ** -0.5,
                                              w[:, at["kn_g"]:at["kn_g"] + 1], ALU.mult, ALU.mult))
                chain(nc.vector.memset(mv[:, :, :], 1.0))
                chain(nc.vector.memset(mrow[:, :], 0.0))
                dve.wait_ge(zT_turned, 1)
                nc.vector.tensor_copy(L.zT[:, 1, :], wide[:, 1, :]).then_inc(zT_ready, 1)
                ctx_stats(dve, chain, 0)
                ctx_norm(dve, 0)
                for p in range(NQ):
                    bank = (bS, bO)[p % 2]
                    half = sc[:, (p % 2) * N:(p % 2 + 1) * N]
                    dve.wait_ge(q_meaned, p + 1)
                    if p >= 2:
                        dve.wait_ge(q_ready, p - 1)
                    nc.vector.tensor_scalar(half, bank[:, :], 1e-16, None, ALU.max).then_inc(q_clamped, 1)
                    dve.wait_ge(q_rnorm, 2 * p + 2)
                    nc.vector.scalar_tensor_tensor(qT[:, p, :], wide[:, p % 4, :], gq[:, 0:1], half,
                                                   ALU.mult, ALU.mult).then_inc(q_ready, 1)

                def key_copy(b, p):
                    for h in range(2):
                        ps, a, n = span(h)
                        dve.wait_ge(k_projected, (b * NQ + p) * 2 + h + 1)
                        nc.vector.tensor_copy(kn[:, p % 2, a:a + n], ps).then_inc(k_copied, 1)

                def key_clamp(b, p):
                    for h in range(2):
                        ps, a, n = span(h)
                        dve.wait_ge(k_meaned, (b * NQ + p) * 2 + h + 1)
                        nc.vector.tensor_scalar(sq[:, a:a + n], ps, 1e-16, None, ALU.max).then_inc(k_clamped, 1)

                def score_max(b, p):
                    for h in range(2):
                        ps, a, n = span(h)
                        dve.wait_ge(scored, (b * NQ + p) * 2 + h + 1)
                        take_wait(L, h)
                        nc.vector.tensor_tensor_reduce(sc[:, a:a + n], ps, mrow[:, a:a + n], 1.0, -3.0e38,
                                                       ALU.add, ALU.max, mx[:, h:h + 1]).then_inc(s_taken, 1)
                    dve.wait_ge(s_taken, (b * NQ + p) * 2 + 2)
                    nc.vector.tensor_reduce(nm[:, :], mx[:, :], AX.X, ALU.max, negate=True).then_inc(shifted, 1)
                    dve.wait_ge(shifted, b * NQ + p + 1)

                def weights_turned(b, p):
                    for g in (1, 3):
                        a, n = GROUPS[g]
                        dve.wait_ge(turned, (b * NQ + p) * len(GROUPS) + g + 1)
                        if g == 1:
                            nc.vector.tensor_copy(pT[:, a:a + n, :], bT[:, 1, :].rearrange("p (a n) -> p a n", n=P)
                                                  ).then_inc(pT_odd, 1)
                        else:
                            for t in range(a, a + n):
                                r = rows(t)
                                last = nc.vector.tensor_copy(pT[0:r, t, :], bT[0:r, 1, (t - a) * P:(t - a + 1) * P])
                            last.then_inc(pT_odd, 1)

                def invert_sum(b, p):
                    dve.wait_ge(exp_ready, b * NQ + p + 1)
                    nc.vector.reciprocal(rs[:, p % 2:p % 2 + 1], sm[:, :]).then_inc(sum_inverted, 1)

                def divide(b, p):
                    dve.wait_ge(sum_inverted, b * NQ + p + 1)
                    dve.wait_ge(mixed, b * NQ + p + 1)
                    nc.vector.tensor_scalar(oh[:, :], bS[:, 0:D], rs[:, p % 2:p % 2 + 1], None, ALU.mult).then_inc(oh_ready, 1)

                def keep_result(b, p):
                    dve.wait_ge(v_applied, b * NQ + p + 1)
                    take_wait(L, 2)
                    nc.vector.tensor_copy(qT[:, p, bass.ds(b * S, S)], bS[:, 256:256 + S]).then_inc(att_ready, 1)

                def batch(b, last_batch):
                    dve.wait_ge(mask_loaded, 16 * b + 16)
                    chain(nc.vector.tensor_copy(mrow[:, 0:CTX], mrow8[:, :]))
                    nc.vector.tensor_scalar(mrow[:, 0:CTX], mrow[:, 0:CTX], 1.0, 1e30, ALU.subtract, ALU.mult
                                            ).then_inc(mask_ready, 1)
                    dve.wait_ge(mask_ready, b + 1)
                    dve.wait_ge(q_ready, NQ)
                    nc.vector.tensor_tensor(qd[:, :, :, :],
                                            qT[:, :, bass.ds(b * S, S)].unsqueeze(2).broadcast_to([P, NQ, 2, S]),
                                            L.half.unsqueeze(1).unsqueeze(3).broadcast_to([P, NQ, 2, S]),
                                            ALU.mult).then_inc(qd_ready, 1)
                    dve.wait_ge(qd_ready, b + 1)
                    dve.wait_ge(latents_moved, 32)
                    nc.vector.tensor_copy(xn[0:S, CT, :], ln64[:, bass.ds(b, 1), :].squeeze(1)).then_inc(xn_ready, 1)
                    nc.vector.tensor_copy(xnT[:, :, CTX:KC], L.zT[:, :, bass.ds(b * S, S)]).then_inc(xT_dve, 1)
                    for g in range(4):
                        a, n = GROUPS[g][0], min(GROUPS[g][1], CT - GROUPS[g][0])
                        dve.wait_ge(xn_turned, 8 * b + 5 + g)
                        c = min(n * P, CTX - a * P)
                        nc.vector.tensor_copy(xnT[:, 1, a * P:a * P + c], wide[:, g, 0:c]).then_inc(xT_dve, 1)
                    key_copy(b, 0)
                    key_clamp(b, 0)
                    for p in range(NQ):
                        if p + 1 < NQ:
                            key_copy(b, p + 1)
                        score_max(b, p)
                        if p >= 1:
                            divide(b, p - 1)
                        if p + 1 < NQ:
                            key_clamp(b, p + 1)
                        invert_sum(b, p)
                        weights_turned(b, p)
                        if p >= 1:
                            keep_result(b, p - 1)
                        if not last_batch:
                            if p == 2:
                                ctx_stats(dve, chain, b + 1)
                            if p == 4:
                                ctx_norm(dve, b + 1)
                    divide(b, NQ - 1)
                    keep_result(b, NQ - 1)
                with dve.Fori(0, B - 1) as b:
                    with chain.loop(b, B - 1, 1 + 2):
                        batch(b, False)
                batch(B - 1, True)
                dve.wait_ge(projected, 1)
                chain(nc.vector.tensor_tensor(L.x[:, :, :], L.x[:, :, :],
                                              wide[:, 0:2, :].rearrange("p a (b n) -> p (a b) n", n=D), ALU.add))
                chain(nc.vector.tensor_tensor(L.x[:, :, :], L.x[:, :, :],
                                              w[:, at["bout"]:at["bout"] + D].unsqueeze(1).broadcast_to([P, NT, D]),
                                              ALU.add))

            @block.gpsimd
            def _(pool):
                pool.wait_ge(w_ready[0], w_ready[1])
                with pool.Fori(0, B) as b:
                    pool.wait_ge(ctx_normed, b + 1)
                    pool.wait_ge(mixed, NQ * b)
                    for n, (o, op, done) in enumerate((("ln_x_g", ALU.mult, gained), ("ln_x_b", ALU.add, xn_ready))):
                        if n:
                            pool.wait_ge(gained, 2 * b + 2)
                        for a, c, r in ((0, CT - 1, P), (CT - 1, 1, CLAST)):
                            src = (raw if n == 0 else xn)[0:r, a:a + c, :]
                            gb = w[0:r, at[o]:at[o] + D].unsqueeze(1).broadcast_to([r, c, D])
                            nc.gpsimd.tensor_tensor(xn[0:r, a:a + c, :], src, gb, op).then_inc(done, 1)
                    for p in range(NQ):
                        for h in range(2):
                            a, n = SPAN[h]
                            pool.wait_ge(k_rnorm, (b * NQ + p) * 4 + h + 3)
                            nc.gpsimd.tensor_tensor(kn[:, p % 2, a:a + n], kn[:, p % 2, a:a + n], sq[:, a:a + n],
                                                    ALU.mult).then_inc(kn_ready, 1)

            @block.scalar
            def _(act):
                norm_scalar(L, act, ln_stats_ready, rstd_ready)
                norm_scalar(L, act, ln_stats_ready, rstd_ready, nx=1)
                act.wait_ge(zT_turned, 1)
                nc.scalar.activation(L.zT[:, 0, :], wide[:, 0, :], ACT.Copy).then_inc(zT_ready, 1)

                def ctx_rstd(b):
                    act.wait_ge(ctx_var_ready, b + 1)
                    nc.scalar.activation(ve[:, :], ve[:, :], ACT.Ln).then_inc(ctx_rstd_ready, 1)
                    act.wait_ge(ctx_rstd_ready, 2 * b + 1)
                    nc.scalar.activation(ve[:, :], ve[:, :], ACT.Exp, scale=-0.5).then_inc(ctx_rstd_ready, 1)
                ctx_rstd(0)
                for p in range(NQ):
                    act.wait_ge(q_projected, p + 1)
                    if p >= 1:
                        act.wait_ge(q_meaned, p)
                    nc.scalar.activation(sq[:, 0:N], wide[:, p % 4, :], ACT.Square).then_inc(q_squared, 1)
                    half = sc[:, (p % 2) * N:(p % 2 + 1) * N]
                    act.wait_ge(q_clamped, p + 1)
                    nc.scalar.activation(half, half, ACT.Ln).then_inc(q_rnorm, 1)
                    act.wait_ge(q_rnorm, 2 * p + 1)
                    nc.scalar.activation(half, half, ACT.Exp, scale=-0.5).then_inc(q_rnorm, 1)

                def key_square(b, p):
                    act.wait_ge(kn_ready, (b * NQ + p) * 2)
                    for h in range(2):
                        ps, a, n = span(h)
                        act.wait_ge(k_copied, (b * NQ + p) * 2 + h + 1)
                        nc.scalar.activation(sq[:, a:a + n], kn[:, p % 2, a:a + n], ACT.Square
                                             ).then_inc(k_squared, 1)

                def key_rnorm(b, p):
                    for h, (a, n) in enumerate(SPAN):
                        act.wait_ge(k_clamped, (b * NQ + p) * 2 + h + 1)
                        nc.scalar.activation(sq[:, a:a + n], sq[:, a:a + n], ACT.Ln).then_inc(k_rnorm, 1)
                    for h, (a, n) in enumerate(SPAN):
                        act.wait_ge(k_rnorm, (b * NQ + p) * 4 + h + 1)
                        nc.scalar.activation(sq[:, a:a + n], sq[:, a:a + n], ACT.Exp, scale=-0.5).then_inc(k_rnorm, 1)

                def mixed_out(b, p):
                    act.wait_ge(oh_turned, b * NQ + p + 1)
                    nc.scalar.activation(ohT[:, :, :], bO[:, 0:KT * P].rearrange("p (a n) -> p a n", n=P),
                                         ACT.Copy).then_inc(ohT_ready, 1)

                def batch(b, last_batch):
                    for g in range(4):
                        a, n = GROUPS[g][0], min(GROUPS[g][1], CT - GROUPS[g][0])
                        act.wait_ge(xn_turned, 8 * b + 1 + g)
                        c = min(n * P, CTX - a * P)
                        nc.scalar.activation(xnT[:, 0, a * P:a * P + c], wide[:, g, 0:c], ACT.Copy).then_inc(xT_act, 1)
                    key_square(b, 0)
                    key_rnorm(b, 0)
                    for p in range(NQ):
                        if p + 1 < NQ:
                            key_square(b, p + 1)
                        act.wait_ge(shifted, b * NQ + p + 1)
                        act.wait_ge(sum_inverted, b * NQ + p)
                        nc.scalar.activation(sc[:, :], sc[:, :], ACT.Exp, bias=nm[:, 0:1], accum_out=sm[:, 0:1]
                                             ).then_inc(exp_ready, 1)
                        if p + 1 < NQ:
                            key_rnorm(b, p + 1)
                        if p >= 1:
                            mixed_out(b, p - 1)
                        for g in (0, 2):
                            a, n = GROUPS[g]
                            act.wait_ge(turned, (b * NQ + p) * len(GROUPS) + g + 1)
                            nc.scalar.activation(pT[:, a:a + n, :], bT[:, 0, :].rearrange("p (a n) -> p a n", n=P),
                                                 ACT.Copy).then_inc(pT_even, 1)
                        if not last_batch and p == 2:
                            ctx_rstd(b + 1)
                    mixed_out(b, NQ - 1)
                with act.Fori(0, B - 1) as b:
                    batch(b, False)
                batch(B - 1, True)

            @block.tensor
            def _(pe):
                pe.wait_ge(latents_ready, 1)
                turn_tensor(L, wide).then_inc(zT_turned, 1)
                pe.wait_ge(zT_ready, 2)
                pe.wait_ge(w_ready[0], w_ready[1])
                for p in range(NQ):
                    if p >= 4:
                        pe.wait_ge(q_ready, p - 3)
                    for k in range(KT):
                        last = nc.tensor.matmul(wide[:, p % 4, :], wq[:, k, p * P:(p + 1) * P], L.zT[:, k, :],
                                                start=(k == 0), stop=(k == KT - 1))
                    last.then_inc(q_projected, 1)
                    pe.wait_ge(q_squared, p + 1)
                    if p >= 2:
                        pe.wait_ge(q_ready, p - 1)
                    nc.tensor.matmul((bS, bO)[p % 2][:, :], blk, sq[:, 0:N], start=True, stop=True
                                     ).then_inc(q_meaned, 1)

                def keys(b, p):
                    for h in range(2):
                        if p >= 1:
                            pe.wait_ge(k_clamped, (b * NQ + p - 1) * 2 + h + 1)
                        for c, (a, n) in enumerate(HALVES[h]):
                            for k in range(KT):
                                last = nc.tensor.matmul(wide[:, 2 * h + c, 0:n], wk[:, k, p * P:(p + 1) * P],
                                                        xnT[:, k, a:a + n], start=(k == 0), stop=(k == KT - 1))
                        last.then_inc(k_projected, 1)

                def means(b, p):
                    for h in range(2):
                        pe.wait_ge(k_squared, (b * NQ + p) * 2 + h + 1)
                        pe.wait_ge(k_copied, (b * NQ + p) * 2 + h + 1)
                        if p >= 1:
                            pe.wait_ge(s_taken, (b * NQ + p - 1) * 2 + h + 1)
                        for c, (a, n) in enumerate(HALVES[h]):
                            last = nc.tensor.matmul(wide[:, 2 * h + c, 0:n], blk, sq[:, a:a + n], start=True, stop=True)
                        last.then_inc(k_meaned, 1)

                def scores(b, p):
                    for h in range(2):
                        if p + 1 < NQ:
                            pe.wait_ge(k_copied, (b * NQ + p + 1) * 2 + h + 1)
                        else:
                            pe.wait_ge(k_clamped, (b * NQ + p) * 2 + h + 1)
                        pe.wait_ge(kn_ready, (b * NQ + p) * 2 + h + 1)
                        for c, (a, n) in enumerate(HALVES[h]):
                            last = nc.tensor.matmul(wide[:, 2 * h + c, 0:n],
                                                    qd[:, p, :, :].rearrange("p a s -> p (a s)"),
                                                    kn[:, p % 2, a:a + n], start=True, stop=True)
                        last.then_inc(scored, 1)

                def turn_weights(b, p):
                    pe.wait_ge(exp_ready, b * NQ + p + 1)
                    for g, (a, n) in enumerate(GROUPS):
                        if g == 2:
                            pe.wait_ge(pT_even, (b * NQ + p) * 2 + 1)
                        if g == 3:
                            pe.wait_ge(pT_odd, (b * NQ + p) * 2 + 1)
                        for t in range(a, a + n):
                            r = rows(t)
                            last = nc.tensor.transpose(bT[0:r, g % 2, (t - a) * P:(t - a + 1) * P],
                                                       sc[:, start(t):start(t) + r], L.ident)
                        last.then_inc(turned, 1)

                def mix(b, p):
                    pe.wait_ge(pT_even, (b * NQ + p) * 2 + 2)
                    pe.wait_ge(pT_odd, (b * NQ + p) * 2 + 2)
                    pe.wait_ge(att_ready, b * NQ + p)
                    for t in range(TILES):
                        r = rows(t)
                        last = nc.tensor.matmul(bS[:, 0:D], pT[0:r, t, :], xn[0:r, t, :],
                                                start=(t == 0), stop=(t == TILES - 1))
                    last.then_inc(mixed, 1)

                def turn_mixed(b, p):
                    pe.wait_ge(oh_ready, b * NQ + p + 1)
                    for k in range(KT):
                        last = nc.tensor.transpose(bO[:, k * P:(k + 1) * P], oh[:, k * P:(k + 1) * P], L.ident)
                    last.then_inc(oh_turned, 1)

                def apply_v(b, p):
                    pe.wait_ge(ohT_ready, b * NQ + p + 1)
                    for h in range(2):
                        c = (2 * p + h) * DH
                        for k in range(KT):
                            last = nc.tensor.matmul(bS[h * DH:(h + 1) * DH, 256:256 + S], wv[:, k, c:c + DH],
                                                    ohT[:, k, h * S:(h + 1) * S], start=(k == 0), stop=(k == KT - 1))
                    last.then_inc(v_applied, 1)

                with pe.Fori(0, B) as b:
                    pe.wait_ge(xn_ready, 3 * b + 3)
                    pe.wait_ge(s_taken, 2 * NQ * b)
                    pe.wait_ge(q_ready, NQ)
                    for k in range(KT):
                        for g in range(4):
                            a, n = GROUPS[g][0], min(GROUPS[g][1], CT - GROUPS[g][0])
                            if k:
                                pe.wait_ge(xT_act, 4 * b + g + 1)
                            for t in range(a, a + n):
                                r = rows(t)
                                last = nc.tensor.transpose(wide[:, g, (t - a) * P:(t - a) * P + r],
                                                           xn[0:r, t, k * P:(k + 1) * P], L.ident[0:r, 0:r])
                            last.then_inc(xn_turned, 1)
                    pe.wait_ge(xT_dve, 5 * b + 5)
                    pe.wait_ge(qd_ready, b + 1)
                    keys(b, 0)
                    means(b, 0)
                    for p in range(NQ):
                        if p + 1 < NQ:
                            keys(b, p + 1)
                        scores(b, p)
                        if p >= 1:
                            mix(b, p - 1)
                        if p + 1 < NQ:
                            means(b, p + 1)
                        if p >= 1:
                            turn_mixed(b, p - 1)
                        turn_weights(b, p)
                        if p >= 1:
                            apply_v(b, p - 1)
                    mix(b, NQ - 1)
                    turn_mixed(b, NQ - 1)
                    apply_v(b, NQ - 1)
                pe.wait_ge(att_ready, NQ * B)
                for t in range(NT):
                    for k in range(NQ):
                        last = nc.tensor.matmul(wide[:, t // 2, (t % 2) * D:(t % 2 + 1) * D],
                                                qT[:, k, t * P:(t + 1) * P], wo[:, k, :],
                                                start=(k == 0), stop=(k == NQ - 1))
                last.then_inc(projected, 1)
        end_layer(nc, sems)


def l1_xattn(L, nc, w, w_ready, at):
    name = "L1_xattn_"
    with ExitStack() as ctx:
        sems = []

        def sb(n, shape, dt=F32):
            return ctx.enter_context(nc.sbuf_tensor(name + n, shape, dt))

        def sem(n):
            s = ctx.enter_context(nc.semaphore(name + n))
            sems.append(s)
            return s
        wide, bS, bO, bT = psum4(nc, ctx, name)
        wq, wk, wv, wo = (w[:, at[n]:at[n] + KT * D].rearrange("p (k n) -> p k n", k=KT)
                          for n in ("wq", "wk", "wv", "wo"))
        cT = sb("ctx_feat", [P, KT, CTX])
        kT = sb("kT", [P, KT, CTX])
        V = sb("V", [P, CT, D])
        mk = sb("mask", [P, CTX])
        qT = sb("qT", [P, KT, N])
        qd = sb("q_by_head", [P, KT, 8, S])
        hs = sb("head_scale", [P, 8])
        sc = sb("scores", [P, 2, CTX])
        mx = sb("max", [P, 2])
        nm = sb("neg_max", [P, 2])
        sm = sb("sum", [P, NP_])
        pT = sb("probsT", [P, 2, CT, P])
        om = sb("out_by_head", [P, NP_, 32])
        aT = sb("attT", [P, KT, N])
        dve_chain = sem("dve_chain")
        ln_stats_ready = sem("ln_stats_ready")
        rstd_ready = sem("rstd_ready")
        z_ready = sem("z_ready")
        zT_turned = sem("zT_turned")
        zT_ready = sem("zT_ready")
        q_projected = sem("q_projected")
        q_ready = sem("q_ready")
        mask_loaded = sem("mask_loaded")
        ctx_loaded = sem("ctx_loaded")
        unit_projected = sem("unit_projected")
        k_ready = sem("k_ready")
        v_ready = sem("v_ready")
        qd_ready = sem("qd_ready")
        scored = sem("scored")
        s_taken = sem("scores_taken")
        shifted = sem("shifted")
        exp_ready = sem("exp_ready")
        turned = sem("probs_turned")
        pT_even = sem("probsT_even_ready")
        pT_odd = sem("probsT_odd_ready")
        pv_done = sem("pv_done")
        om_ready = sem("om_ready")
        merged = sem("merged")
        att_ready = sem("att_ready")
        projected = sem("projected")
        HALVES = [(0, 1024), (1024, CTX - 1024)]
        GROUPS = [(0, 4), (4, 4), (8, 4), (12, 1)]
        KU, VU = KT * len(CHUNKS), -(-CT // 2)
        U = KU + VU
        with nc.Block() as block:
            @block.sync
            def _(sp):
                for h in range(2):
                    sp.dma_start(mk[h * S:(h + 1) * S, :], L.aps["mask_SS2"]).then_inc(mask_loaded, 16)
                with sp.Fori(0, B) as b:
                    sp.wait_ge(unit_projected, U * b)
                    sp.dma_start(cT[:, :, :], L.aps["ctx_feat"][bass.ds(b, 1)].squeeze(0)
                                 .rearrange("(k p) n -> p k n", p=P)).then_inc(ctx_loaded, 16)

            @block.vector
            def _(dve):
                chain = Chain(dve, dve_chain)
                norm_vector(L, dve, chain, ln_stats_ready, rstd_ready, z_ready)
                dve.wait_ge(zT_turned, 1)
                nc.vector.tensor_copy(L.zT[:, 1, :], wide[:, 1, :]).then_inc(zT_ready, 1)
                chain(nc.vector.tensor_scalar(hs[:, :], L.heads8, HD ** -0.5, None, ALU.mult))
                dve.wait_ge(mask_loaded, 32)
                chain(nc.vector.tensor_scalar(mk[:, :], mk[:, :], -1e9, None, ALU.mult))
                dve.wait_ge(q_ready, KT)
                with dve.Fori(0, B) as b:
                    with chain.loop(b, B, 2):
                        for k in range(KT):
                            last = nc.vector.tensor_tensor(
                                qd[:, k, :, :],
                                qT[:, k, bass.ds(b * S, S)].unsqueeze(1).broadcast_to([P, 8, S]),
                                hs[:, :].unsqueeze(2).broadcast_to([P, 8, S]), ALU.mult)
                        last.then_inc(qd_ready, 1)
                        for v in range(VU):
                            u = KU + v
                            n = min(2, CT - 2 * v)
                            r = tile_rows(2 * v)
                            dve.wait_ge(unit_projected, b * U + u + 1)
                            nc.vector.tensor_copy(V[0:r, 2 * v:2 * v + n, :],
                                                  wide[0:r, u % 4, 0:n * D].rearrange("p (a n) -> p a n", n=D)
                                                  ).then_inc(v_ready, 1)
                        def score_max(p):
                            for h, (a, n) in enumerate(HALVES):
                                dve.wait_ge(scored, b * 2 * NP_ + 2 * p + h + 1)
                                if h == 0 and p >= 2:
                                    dve.wait_ge(turned, (b * NP_ + p - 1) * len(GROUPS))
                                take_wait(L, h)
                                nc.vector.tensor_tensor_reduce(
                                    sc[:, p % 2, a:a + n],
                                    wide[:, 2 * h:2 * h + 2, :].rearrange("p a n -> p (a n)")[:, 0:n],
                                    mk[:, a:a + n], 1.0, -3.0e38, ALU.add, ALU.max, mx[:, h:h + 1]
                                ).then_inc(s_taken, 1)
                            dve.wait_ge(s_taken, b * 2 * NP_ + 2 * p + 2)
                            nc.vector.tensor_reduce(nm[:, p % 2:p % 2 + 1], mx[:, :], AX.X, ALU.max, negate=True
                                                    ).then_inc(shifted, 1)
                            dve.wait_ge(shifted, b * NP_ + p + 1)
                        score_max(0)
                        for p in range(NP_):
                            if p + 1 < NP_:
                                score_max(p + 1)
                            for g in (1, 3):
                                a, n = GROUPS[g]
                                r = tile_rows(a)
                                dve.wait_ge(turned, (b * NP_ + p) * len(GROUPS) + g + 1)
                                nc.vector.tensor_copy(pT[0:r, p % 2, a:a + n, :],
                                                      bT[0:r, 1, 0:n * P].rearrange("p (a n) -> p a n", n=P)
                                                      ).then_inc(pT_odd, 1)
                        chain(nc.vector.reciprocal(sm[:, :], sm[:, :]))
                        dve.wait_ge(pv_done, b + 1)
                        chain(nc.vector.tensor_tensor(om[:, :, :],
                                                      bO[:, 0:NP_ * 32].rearrange("p (a s) -> p a s", s=32),
                                                      sm[:, :].unsqueeze(2).broadcast_to([P, NP_, 32]), ALU.mult))
                        nc.vector.tensor_tensor(om[:, :, :], om[:, :, :],
                                                L.pairblk.unsqueeze(1).broadcast_to([P, NP_, 32]),
                                                ALU.mult).then_inc(om_ready, 1)
                dve.wait_ge(projected, 1)
                chain(nc.vector.tensor_tensor(L.x[:, :, :], L.x[:, :, :],
                                              wide[:, 0:2, :].rearrange("p a (b n) -> p (a b) n", n=D), ALU.add))
                chain(nc.vector.tensor_tensor(L.x[:, :, :], L.x[:, :, :],
                                              w[:, at["bo"]:at["bo"] + D].unsqueeze(1).broadcast_to([P, NT, D]),
                                              ALU.add))

            @block.scalar
            def _(act):
                norm_scalar(L, act, ln_stats_ready, rstd_ready)
                act.wait_ge(zT_turned, 1)
                nc.scalar.activation(L.zT[:, 0, :], wide[:, 0, :], ACT.Copy).then_inc(zT_ready, 1)
                for m in range(KT):
                    act.wait_ge(q_projected, m + 1)
                    nc.scalar.activation(qT[:, m, :], wide[:, 2 + m, :], ACT.Identity,
                                         bias=w[:, at["bq"] + m:at["bq"] + m + 1]).then_inc(q_ready, 1)
                with act.Fori(0, B) as b:
                    for u in range(KU):
                        m, c = divmod(u, len(CHUNKS))
                        a, n = CHUNKS[c]
                        act.wait_ge(unit_projected, b * U + u + 1)
                        nc.scalar.activation(kT[:, m, a:a + n], wide[:, u % 4, 0:n], ACT.Identity,
                                             bias=w[:, at["bk"] + m:at["bk"] + m + 1]).then_inc(k_ready, 1)
                    def exponentials(p):
                        act.wait_ge(shifted, b * NP_ + p + 1)
                        nc.scalar.activation(sc[:, p % 2, :], sc[:, p % 2, :], ACT.Exp, bias=nm[:, p % 2:p % 2 + 1],
                                             accum_out=sm[:, p:p + 1]).then_inc(exp_ready, 1)

                    def copy_turned(p, g):
                        a, n = GROUPS[g]
                        act.wait_ge(turned, (b * NP_ + p) * len(GROUPS) + g + 1)
                        nc.scalar.activation(pT[:, p % 2, a:a + n, :],
                                             bT[:, 0, :].rearrange("p (a n) -> p a n", n=P),
                                             ACT.Copy).then_inc(pT_even, 1)
                    exponentials(0)
                    for p in range(NP_):
                        copy_turned(p, 0)
                        if p + 1 < NP_:
                            exponentials(p + 1)
                        copy_turned(p, 2)
                    act.wait_ge(merged, b + 1)
                    for m in range(KT):
                        nc.scalar.activation(aT[:, m, bass.ds(b * S, S)], bS[:, m * S:(m + 1) * S], ACT.Identity,
                                             bias=w[:, at["bv"] + m:at["bv"] + m + 1]).then_inc(att_ready, 1)

            @block.tensor
            def _(pe):
                pe.wait_ge(z_ready, 1)
                turn_tensor(L, wide).then_inc(zT_turned, 1)
                pe.wait_ge(w_ready[0], w_ready[1])
                pe.wait_ge(zT_ready, 2)
                for m in range(KT):
                    for k in range(KT):
                        last = nc.tensor.matmul(wide[:, 2 + m, :], wq[:, k, m * P:(m + 1) * P],
                                                L.zT[:, k, :], start=(k == 0), stop=(k == KT - 1))
                    last.then_inc(q_projected, 1)
                pe.wait_ge(q_ready, KT)
                with pe.Fori(0, B) as b:
                    pe.wait_ge(ctx_loaded, 16 * b + 16)
                    pe.wait_ge(s_taken, b * 2 * NP_)
                    for u in range(U):
                        if u - 4 >= KU:
                            pe.wait_ge(v_ready, b * VU + u - 4 - KU + 1)
                        elif u >= 4:
                            pe.wait_ge(k_ready, b * KU + u - 3)
                        if u < KU:
                            m, c = divmod(u, len(CHUNKS))
                            a, n = CHUNKS[c]
                            for k in range(KT):
                                last = nc.tensor.matmul(wide[:, u % 4, 0:n], wk[:, k, m * P:(m + 1) * P],
                                                        cT[:, k, a:a + n], start=(k == 0), stop=(k == KT - 1))
                        else:
                            for t in range(2 * (u - KU), min(2 * (u - KU) + 2, CT)):
                                r = tile_rows(t)
                                for k in range(KT):
                                    last = nc.tensor.matmul(wide[0:r, u % 4, (t % 2) * D:(t % 2 + 1) * D],
                                                            cT[:, k, t * P:t * P + r], wv[:, k, :],
                                                            start=(k == 0), stop=(k == KT - 1))
                        last.then_inc(unit_projected, 1)
                    pe.wait_ge(k_ready, b * KU + KU)
                    pe.wait_ge(v_ready, b * VU + VU)
                    pe.wait_ge(qd_ready, b + 1)

                    def scores(p):
                        k, j = p // 4, p % 4
                        for h, (a, n) in enumerate(HALVES):
                            if p >= 1:
                                pe.wait_ge(s_taken, b * 2 * NP_ + 2 * p - 1 + h)
                            for c in range(2):
                                ca, cn = CHUNKS[2 * h + c]
                                last = nc.tensor.matmul(wide[:, 2 * h + c, 0:cn], qd[:, k, 2 * j:2 * j + 2, :],
                                                        kT[:, k, ca:ca + cn], start=True, stop=True)
                            last.then_inc(scored, 1)

                    def turn_group(p, g):
                        a, n = GROUPS[g]
                        if g == 2:
                            pe.wait_ge(pT_even, (b * NP_ + p) * 2 + 1)
                        if g == 3:
                            pe.wait_ge(pT_odd, (b * NP_ + p) * 2 + 1)
                        if g == 0 and p >= 1:
                            pe.wait_ge(pT_even, (b * NP_ + p) * 2)
                        if g == 1 and p >= 1:
                            pe.wait_ge(pT_odd, (b * NP_ + p) * 2)
                        for t in range(a, a + n):
                            r = tile_rows(t)
                            last = nc.tensor.transpose(bT[0:r, g % 2, (t - a) * P:(t - a + 1) * P],
                                                       sc[:, p % 2, t * P:t * P + r], L.ident)
                        last.then_inc(turned, 1)

                    def weigh(p):
                        pe.wait_ge(pT_even, (b * NP_ + p) * 2 + 2)
                        pe.wait_ge(pT_odd, (b * NP_ + p) * 2 + 2)
                        for t in range(CT):
                            r = tile_rows(t)
                            last = nc.tensor.matmul(bO[:, p * 32:(p + 1) * 32], pT[0:r, p % 2, t, :],
                                                    V[0:r, t, 32 * p:32 * p + 32], start=(t == 0), stop=(t == CT - 1))
                        return last
                    scores(0)
                    for p in range(NP_):
                        if p + 1 < NP_:
                            scores(p + 1)
                        pe.wait_ge(exp_ready, b * NP_ + p + 1)
                        turn_group(p, 0)
                        turn_group(p, 1)
                        if p >= 1:
                            weigh(p - 1)
                        turn_group(p, 2)
                        turn_group(p, 3)
                    last = weigh(NP_ - 1)
                    last.then_inc(pv_done, 1)
                    pe.wait_ge(om_ready, b + 1)
                    pe.wait_ge(att_ready, KT * b)
                    for k in range(KT):
                        last = nc.tensor.matmul(bS[:, k * S:(k + 1) * S],
                                                om[:, 4 * k:4 * k + 4, :].rearrange("p a s -> p (a s)"),
                                                L.fold, start=True, stop=True)
                    last.then_inc(merged, 1)
                pe.wait_ge(att_ready, KT * B)
                for t in range(NT):
                    for k in range(KT):
                        last = nc.tensor.matmul(wide[:, t // 2, (t % 2) * D:(t % 2 + 1) * D],
                                                aT[:, k, t * P:(t + 1) * P], wo[:, k, :],
                                                start=(k == 0), stop=(k == KT - 1))
                last.then_inc(projected, 1)
        end_layer(nc, sems)


def l3_xattn(L, nc, w, w_ready, at):
    name = "L3_xattn_"
    G16 = D // HD
    with ExitStack() as ctx:
        sems = []

        def sb(n, shape, dt=F32):
            return ctx.enter_context(nc.sbuf_tensor(name + n, shape, dt))

        def sem(n):
            s = ctx.enter_context(nc.semaphore(name + n))
            sems.append(s)
            return s
        wide, bS, bO, bT = psum4(nc, ctx, name)
        wq, wk, wv, wp = (w[:, at[n]:at[n] + KT * D].rearrange("p (k n) -> p k n", k=KT)
                          for n in ("Wq", "Wk", "Wv", "Wp"))
        blk = L.const[:, C_BLK16:C_BLK16 + P]
        cT = sb("ctx_feat", [P, 2, KT, CTX])
        ck = sb("ctx_tok", [P, 2, CT, D])
        q = sb("q_tok", [P, NT, D])
        qT = sb("qT", [P, KT, N])
        ks = sb("k_tok", [P, 2, CT, D])
        g16 = sb("group_max", [P, 4, G16])
        r16 = sb("group_rsum", [P, 4, G16])
        GT = sb("ctx_by_k", [P, KT, D])
        kc = sb("k_sum", [P, KT])
        kv = sb("kv", [P, KT, P])
        kcb = sb("k_sum_block", [P, KT, P])
        rd = sb("rden", [P, KT, S])
        oT = sb("outT", [P, KT, N])
        one = sb("ones", [P, 1])
        dve_chain = sem("dve_chain")
        ln_stats_ready = sem("ln_stats_ready")
        rstd_ready = sem("rstd_ready")
        z_ready = sem("z_ready")
        zT_turned = sem("zT_turned")
        zT_ready = sem("zT_ready")
        q_projected = sem("q_projected")
        q_shifted = sem("q_shifted")
        q_exp_ready = sem("q_exp_ready")
        q_ready = sem("q_ready")
        q_turned = sem("q_turned")
        qT_ready = sem("qT_ready")
        loaded = [sem("ctx_loaded_0"), sem("ctx_loaded_1")]
        k_projected = sem("k_projected")
        k_taken = sem("k_taken")
        k_shifted = sem("k_shifted")
        k_exp_ready = sem("k_exp_ready")
        k_ready = sem("k_ready")
        ctx_summed = sem("ctx_summed")
        GT_ready = sem("GT_ready")
        kv_projected = sem("kv_projected")
        kv_ready = sem("kv_ready")
        attended = sem("attended")
        oT_ready = sem("oT_ready")
        projected = sem("projected")
        GROUPS = [(0, 4, P), (4, 4, P), (8, 4, P), (12, 1, CLAST)]
        NG = len(GROUPS)

        def group_psum(g):
            a, n, r = GROUPS[g]
            return wide[0:r, 2 * (g % 2):2 * (g % 2) + 2, :].rearrange("p a (b n) -> p (a b) n", n=D)[:, 0:n, :]
        with nc.Block() as block:
            def load(sp, b, j):
                row = lambda a: a[bass.ds(b, 1)].squeeze(0)
                sp.dma_start(cT[:, j, :, :], row(L.aps["ctx_feat"]).rearrange("(k p) n -> p k n", p=P)
                             ).then_inc(loaded[j], 16)
                load_ctx_tok(sp, ck[:, j, :, :], row(L.aps["ctx_tok"]), loaded[j])

            @block.sync
            def _(sp):
                for j in range(2):
                    load(sp, j, j)
                with sp.Fori(0, B // 2 - 1) as i:
                    for j in range(2):
                        sp.wait_ge(ctx_summed, 2 * i + j + 1)
                        load(sp, 2 * i + 2 + j, j)

            def groups_of(a, r, n):
                return a.rearrange("p t (g e) -> p (t g) e", e=HD)

            @block.vector
            def _(dve):
                chain = Chain(dve, dve_chain)
                chain(nc.vector.memset(one[:, :], 1.0))
                norm_vector(L, dve, chain, ln_stats_ready, rstd_ready, z_ready)
                dve.wait_ge(zT_turned, 1)
                nc.vector.tensor_copy(L.zT[:, 1, :], wide[:, 1, :]).then_inc(zT_ready, 1)

                def bias_and_shift(src, dst, bias, r, n, done, taken=None):
                    gm = g16[0:r, 0:n, :].rearrange("p t g -> p (t g)")
                    bb = bias[0:r, :].unsqueeze(1).broadcast_to([r, n, D])
                    ins = nc.vector.tensor_tensor(dst, src, bb, ALU.add)
                    if taken is None:
                        chain(ins)
                    else:
                        ins.then_inc(taken[0], 1)
                        dve.wait_ge(taken[0], taken[1])
                        dve.wait_ge(done, taken[1] - 1)
                    chain(nc.vector.tensor_reduce(gm, groups_of(dst, r, n), AX.X, ALU.max))
                    nc.vector.tensor_tensor(groups_of(dst, r, n), groups_of(dst, r, n),
                                            gm.unsqueeze(2).broadcast_to([r, n * G16, HD]), ALU.subtract
                                            ).then_inc(done, 1)

                def divide(dst, r, n, done, before=None):
                    if before is not None:
                        dve.wait_ge(done, before)
                    rm = r16[0:r, 0:n, :].rearrange("p t g -> p (t g)")
                    chain(nc.vector.tensor_reduce(rm, groups_of(dst, r, n), AX.X, ALU.add))
                    chain(nc.vector.reciprocal(rm, rm))
                    nc.vector.tensor_tensor(groups_of(dst, r, n), groups_of(dst, r, n),
                                            rm.unsqueeze(2).broadcast_to([r, n * G16, HD]), ALU.mult
                                            ).then_inc(done, 1)
                bq = w[:, at["bq"]:at["bq"] + D]
                bk = w[:, at["bk"]:at["bk"] + D]
                dve.wait_ge(q_projected, 1)
                bias_and_shift(wide[:, 2:4, :].rearrange("p a (b n) -> p (a b) n", n=D), q[:, :, :], bq, P, NT,
                               q_shifted)
                dve.wait_ge(q_exp_ready, 1)
                divide(q[:, :, :], P, NT, q_ready)
                dve.wait_ge(q_turned, 1)
                nc.vector.tensor_copy(qT[:, :, :], wide[:, 0:2, :]).then_inc(qT_ready, 1)

                def keys(b, j):
                    for g, (a, n, r) in enumerate(GROUPS):
                        dve.wait_ge(k_projected, b * NG + g + 1)
                        bias_and_shift(group_psum(g), ks[0:r, j, a:a + n, :], bk, r, n, k_shifted,
                                       (k_taken, b * NG + g + 1))
                        if g >= 1:
                            pa, pn, pr = GROUPS[g - 1]
                            dve.wait_ge(k_exp_ready, b * NG + g)
                            divide(ks[0:pr, j, pa:pa + pn, :], pr, pn, k_ready, b * NG + g - 1)
                    dve.wait_ge(k_exp_ready, b * NG + NG)
                    a, n, r = GROUPS[-1]
                    divide(ks[0:r, j, a:a + n, :], r, n, k_ready, b * NG + NG - 1)

                def combine(b):
                    dve.wait_ge(ctx_summed, b + 1)
                    chain(nc.vector.tensor_copy(kc[:, :], bO[:, 0:KT]))
                    nc.vector.tensor_copy(GT[:, :, :], bS[:, :].rearrange("p (a n) -> p a n", n=D)
                                          ).then_inc(GT_ready, 1)
                    dve.wait_ge(kv_projected, b + 1)
                    for m in range(KT):
                        nc_l = nc.vector.scalar_tensor_tensor(
                            kv[:, m, :], w[:, at["bv"] + m * P:at["bv"] + (m + 1) * P], kc[:, m:m + 1],
                            bT[:, 0, m * P:(m + 1) * P], ALU.mult, ALU.add)
                    chain(nc_l)
                    nc.vector.tensor_tensor(kv[:, :, :], kv[:, :, :], blk.unsqueeze(1).broadcast_to([P, KT, P]),
                                            ALU.mult).then_inc(kv_ready, 1)
                    for m in range(KT):
                        nc.vector.tensor_scalar(kcb[:, m, :], blk, kc[:, m:m + 1], None, ALU.mult
                                                ).then_inc(kv_ready, 1)
                    dve.wait_ge(attended, b + 1)
                    chain(nc.vector.reciprocal(rd[:, :, :], bT[:, 1, KT * S:2 * KT * S]
                                               .rearrange("p (a s) -> p a s", s=S)))
                    chain(nc.vector.tensor_tensor(rd[:, :, :], rd[:, :, :],
                                                  bT[:, 1, 0:KT * S].rearrange("p (a s) -> p a s", s=S), ALU.mult))
                    nc.vector.tensor_tensor(oT[:, :, bass.ds(b * S, S)], rd[:, :, :], qT[:, :, bass.ds(b * S, S)],
                                            ALU.add).then_inc(oT_ready, 1)
                keys(0, 0)
                with dve.Fori(0, B // 2 - 1) as i:
                    with chain.loop(i, B // 2 - 1, 2 * (3 * NG + 4)):
                        keys(2 * i + 1, 1)
                        combine(2 * i)
                        keys(2 * i + 2, 0)
                        combine(2 * i + 1)
                keys(B - 1, 1)
                combine(B - 2)
                combine(B - 1)
                dve.wait_ge(projected, 1)
                chain(nc.vector.tensor_tensor(L.x[:, :, :], L.x[:, :, :],
                                              wide[:, 0:2, :].rearrange("p a (b n) -> p (a b) n", n=D), ALU.add))
                chain(nc.vector.tensor_tensor(L.x[:, :, :], L.x[:, :, :],
                                              w[:, at["bp"]:at["bp"] + D].unsqueeze(1).broadcast_to([P, NT, D]),
                                              ALU.add))

            @block.scalar
            def _(act):
                norm_scalar(L, act, ln_stats_ready, rstd_ready)
                act.wait_ge(zT_turned, 1)
                nc.scalar.activation(L.zT[:, 0, :], wide[:, 0, :], ACT.Copy).then_inc(zT_ready, 1)
                act.wait_ge(q_shifted, 1)
                nc.scalar.activation(q[:, :, :], q[:, :, :], ACT.Exp).then_inc(q_exp_ready, 1)
                with act.Fori(0, B // 2) as i:
                    for j in range(2):
                        for g, (a, n, r) in enumerate(GROUPS):
                            act.wait_ge(k_shifted, (2 * i + j) * NG + g + 1)
                            nc.scalar.activation(ks[0:r, j, a:a + n, :], ks[0:r, j, a:a + n, :], ACT.Exp
                                                 ).then_inc(k_exp_ready, 1)

            @block.tensor
            def _(pe):
                pe.wait_ge(z_ready, 1)
                turn_tensor(L, wide).then_inc(zT_turned, 1)
                pe.wait_ge(w_ready[0], w_ready[1])
                pe.wait_ge(zT_ready, 2)
                for t in range(NT):
                    for k in range(KT):
                        last = nc.tensor.matmul(wide[:, 2 + t // 2, (t % 2) * D:(t % 2 + 1) * D],
                                                L.zT[:, k, t * P:(t + 1) * P], wq[:, k, :],
                                                start=(k == 0), stop=(k == KT - 1))
                last.then_inc(q_projected, 1)
                pe.wait_ge(q_ready, 1)
                turn_tensor(L, wide, z=q).then_inc(q_turned, 1)
                pe.wait_ge(qT_ready, 1)

                def keys(b, j, first=False):
                    pe.wait_ge(loaded[j], 48 * (b // 2) + 48 if isinstance(b, int) else j_loaded)
                    for g, (a, n, r) in enumerate(GROUPS):
                        if g >= 2:
                            pe.wait_ge(k_taken, b * NG + g - 1)
                        elif not first:
                            pe.wait_ge(k_taken, b * NG + g - 1)
                        for u in range(n):
                            for k in range(KT):
                                last = nc.tensor.matmul(group_psum(g)[:, u, :], cT[:, j, k, (a + u) * P:(a + u) * P + r],
                                                        wk[:, k, :], start=(k == 0), stop=(k == KT - 1))
                        last.then_inc(k_projected, 1)

                def summed(b, j):
                    pe.wait_ge(GT_ready, b)
                    pe.wait_ge(k_ready, b * NG + NG)
                    for m in range(KT):
                        for t in range(CT):
                            r = tile_rows(t)
                            nc.tensor.matmul(bS[:, m * D:(m + 1) * D], ck[0:r, j, t, m * P:(m + 1) * P],
                                             ks[0:r, j, t, :], start=(t == 0), stop=(t == CT - 1))
                        for t in range(CT):
                            r = tile_rows(t)
                            last = nc.tensor.matmul(bO[:, m:m + 1], ks[0:r, j, t, m * P:(m + 1) * P],
                                                    one[0:r, :], start=(t == 0), stop=(t == CT - 1))
                    last.then_inc(ctx_summed, 1)
                    pe.wait_ge(GT_ready, b + 1)
                    for m in range(KT):
                        for k in range(KT):
                            last = nc.tensor.matmul(bT[:, 0, m * P:(m + 1) * P], GT[:, k, m * P:(m + 1) * P],
                                                    wv[:, k, m * P:(m + 1) * P], start=(k == 0), stop=(k == KT - 1))
                    last.then_inc(kv_projected, 1)
                    pe.wait_ge(kv_ready, 3 * b + 3)
                    for n, lhs in enumerate((kv, kcb)):
                        for m in range(KT):
                            o = (n * KT + m) * S
                            last = nc.tensor.matmul(bT[:, 1, o:o + S], lhs[:, m, :], qT[:, m, bass.ds(b * S, S)],
                                                    start=True, stop=True)
                    last.then_inc(attended, 1)
                    pe.wait_ge(oT_ready, b + 1)
                keys(0, 0, first=True)
                with pe.Fori(0, B // 2 - 1) as i:
                    j_loaded = 48 * i + 48
                    keys(2 * i + 1, 1)
                    summed(2 * i, 0)
                    j_loaded = 48 * i + 96
                    keys(2 * i + 2, 0)
                    summed(2 * i + 1, 1)
                keys(B - 1, 1)
                summed(B - 2, 0)
                summed(B - 1, 1)
                for t in range(NT):
                    for k in range(KT):
                        last = nc.tensor.matmul(wide[:, t // 2, (t % 2) * D:(t % 2 + 1) * D],
                                                oT[:, k, t * P:(t + 1) * P], wp[:, k, :],
                                                start=(k == 0), stop=(k == KT - 1))
                last.then_inc(projected, 1)
        end_layer(nc, sems)


NSTATE = 16
NCONV = 4


def mamba(L, nc, name, w, at, w_ready, DI, R, b_row, turns, twice):
    MT = DI // P
    with ExitStack() as ctx:
        sems = []

        def sb(n, shape, dt=F32):
            return ctx.enter_context(nc.sbuf_tensor(name + n, shape, dt))

        def sem(n):
            s = ctx.enter_context(nc.semaphore(name + n))
            sems.append(s)
            return s
        wide, bS, bO, bT = psum4(nc, ctx, name)
        z2 = sb("z_again", [P, NT, D]) if twice else L.z
        zT2 = sb("z_reversed", [P, KT, N]) if twice else None
        up = sb("u_padded", [P, MT, B, NCONV - 1 + S])
        u = sb("u", [P, MT, N])
        dt = sb("dt", [P, MT, N])
        dtz = sb("dt_reset", [P, MT, N])
        du = sb("dt_u", [P, MT, N])
        zg = sb("z_gate", [P, MT, N])
        tmp = sb("tmp", [P, MT, N])
        dbc = sb("dbc", [R, N])
        A = sb("A", [P, MT, NSTATE])
        row = sb("chosen_rows", [R, 2, N])
        ones = sb("ones", [R, P])
        bc = sb("B_and_C", [P, 2, 2, N])
        dA = sb("decay", [P, 2, MT, N])
        dBu = sb("input", [P, 2, MT, N])
        ytok = sb("y_tok_reversed", [P, NT, D]) if twice else None
        dve_chain = sem("dve_chain")
        pool_chain = sem("pool_chain")
        act_chain = sem("act_chain")
        ln_stats_ready = sem("ln_stats_ready")
        rstd_ready = sem("rstd_ready")
        z_ready = sem("z_ready")
        zT_turned = sem("zT_turned")
        zT_ready = sem("zT_ready")
        pads_ready = sem("pads_ready")
        u_projected = sem("u_projected")
        u_copied = sem("u_copied")
        z_projected = sem("z_projected")
        zg_ready = sem("zg_ready")
        conv_done = sem("conv_done")
        u_ready = sem("u_ready")
        dbc_projected = sem("dbc_projected")
        dbc_ready = sem("dbc_ready")
        dt_projected = sem("dt_projected")
        dt_logs_ready = sem("dt_logs_ready")
        dt_ready = sem("dt_ready")
        A_exp_ready = sem("A_exp_ready")
        uD_ready = sem("uD_ready")
        row_ready = sem("row_ready")
        bc_done = sem("bc_done")
        bc_ready = sem("bc_ready")
        dA_ready = sem("dA_ready")
        dBu_ready = sem("dBu_ready")
        scanned = sem("scanned")
        hC_ready = sem("hC_ready")
        y_added = sem("y_added")
        y_ready = sem("y_ready")
        out_projected = sem("out_projected")
        ytok_ready = sem("ytok_ready")
        x_added = sem("x_added")
        n_turned = 1 + len(turns) if twice else 1

        with nc.Block() as block:
            @block.vector
            def _(dve):
                chain = Chain(dve, dve_chain)
                norm_vector(L, dve, chain, ln_stats_ready, rstd_ready, z_ready)
                if twice:
                    dve.wait_ge(z_ready, 1)
                    chain(nc.vector.tensor_tensor(L.x[:, :, :], L.x[:, :, :], L.z[:, :, :], ALU.add))
                    norm_vector(L, dve, chain, ln_stats_ready, rstd_ready, z_ready, x=L.z, z=z2, nx=1)
                dve.wait_ge(w_ready[0], w_ready[1])

                def gain(dst, k):
                    if twice:
                        g, b = at["ln_g"] + k, at["ln_b"] + k
                        return nc.vector.tensor_scalar(dst[:, k, :], wide[:, k, :], w[:, g:g + 1], w[:, b:b + 1],
                                                       ALU.mult, ALU.add)
                    return nc.vector.tensor_copy(dst[:, k, :], wide[:, k, :])
                dve.wait_ge(zT_turned, 1)
                for k in range(KT):
                    gain(L.zT, k).then_inc(zT_ready, 1)
                if twice:
                    dve.wait_ge(zT_turned, 2)
                    for k in range(KT):
                        gain(zT2, k).then_inc(zT_ready, 1)
                chain(nc.vector.memset(ones[:, :], 1.0))
                nc.vector.memset(up[:, :, :, 0:NCONV - 1], 0.0).then_inc(pads_ready, 1)
                for d, pre in enumerate(turns):
                    cw, cb = at[pre + "conv_w"], at[pre + "conv_b"]
                    for m in range(MT):
                        dve.wait_ge(u_copied, d * MT + m + 1)
                        acc = tmp[:, m, :].rearrange("p (b s) -> p b s", s=S)
                        for k in range(NCONV):
                            tap = up[:, m, :, k:k + S]
                            c = cw + m * NCONV + k
                            if k == 0:
                                last = nc.vector.tensor_scalar(acc, tap, w[:, c:c + 1], w[:, cb + m:cb + m + 1],
                                                               ALU.mult, ALU.add)
                            else:
                                last = nc.vector.scalar_tensor_tensor(acc, tap, w[:, c:c + 1], acc,
                                                                      ALU.mult, ALU.add)
                            if k < NCONV - 1:
                                chain(last)
                        last.then_inc(conv_done, 1)
                    dve.wait_ge(u_ready, 2 * d + 1)
                    dve.wait_ge(conv_done, (d + 1) * MT)
                    nc.vector.tensor_tensor(u[:, :, :], u[:, :, :], tmp[:, :, :], ALU.mult).then_inc(u_ready, 1)
                    dve.wait_ge(dt_logs_ready, 4 * MT * (d + 1))
                    dve.wait_ge(u_ready, 2 * d + 2)
                    nc.vector.scalar_tensor_tensor(dt[:, :, :], tmp[:, :, :], 0.0, dt[:, :, :],
                                                   ALU.max, ALU.add).then_inc(dt_ready, 1)
                    dve.wait_ge(dt_ready, 4 * d + 1)
                    nc.vector.tensor_tensor(du[:, :, :], dt[:, :, :], u[:, :, :], ALU.mult).then_inc(dt_ready, 1)
                    dve.wait_ge(zg_ready, 3 * MT * (d + 1))
                    chain(nc.vector.tensor_copy(dtz[:, :, :], dt[:, :, :]))
                    nc.vector.memset(dtz[:, :, :].rearrange("p m (b s) -> p (m b) s", s=S)[:, :, 0:1], 1e30
                                     ).then_inc(dt_ready, 1)
                    dve.wait_ge(A_exp_ready, d + 1)
                    nc.vector.tensor_scalar(A[:, :, :], A[:, :, :], -1.0, None, ALU.mult).then_inc(dt_ready, 1)
                    for m in range(MT):
                        c = at[pre + "D"] + m
                        nc.vector.tensor_scalar(tmp[:, m, :], u[:, m, :], w[:, c:c + 1], None, ALU.mult
                                                ).then_inc(uD_ready, 1)
                    base = d * NSTATE
                    with dve.Fori(0, NSTATE // 2) as i:
                        for j in range(2):
                            n = base + 2 * i + j
                            dve.wait_ge(dA_ready, (n + 1) * MT)
                            dve.wait_ge(dBu_ready, n + 1)
                            nc.vector.tensor_tensor_scan(dBu[:, j, :, :].rearrange("p m n -> p (m n)"),
                                                         dA[:, j, :, :].rearrange("p m n -> p (m n)"),
                                                         dBu[:, j, :, :].rearrange("p m n -> p (m n)"),
                                                         0.0, ALU.mult, ALU.add).then_inc(scanned, 1)
                            dve.wait_ge(scanned, n + 1)
                            nc.vector.tensor_tensor(dBu[:, j, :, :], dBu[:, j, :, :],
                                                    bc[:, j, 1, :].unsqueeze(1).broadcast_to([P, MT, N]),
                                                    ALU.mult).then_inc(hC_ready, 1)
                    dve.wait_ge(y_added, (d + 1) * NSTATE + 1 + d)
                    dve.wait_ge(zg_ready, 3 * MT * (d + 1))
                    nc.vector.tensor_tensor(tmp[:, :, :], wide[:, 0:MT, :], zg[:, :, :], ALU.mult).then_inc(y_ready, 1)
                    dve.wait_ge(out_projected, d + 1 if d == 0 else 3)
                    ps = bT[:, :, :].rearrange("p a (b n) -> p (a b) n", n=D)
                    if d == 1:
                        nc.vector.tensor_tensor(L.x[:, :, :], L.x[:, :, :], ps, ALU.add).then_inc(ytok_ready, 1)
                    else:
                        nc.vector.tensor_tensor(L.x[:, :, :], L.x[:, :, :], ps, ALU.add).then_inc(x_added, 1)
                        dve.wait_ge(x_added, 1)

            @block.scalar
            def _(act):
                norm_scalar(L, act, ln_stats_ready, rstd_ready)
                if twice:
                    norm_scalar(L, act, ln_stats_ready, rstd_ready, nx=1)
                act.wait_ge(w_ready[0], w_ready[1])
                act.wait_ge(pads_ready, 1)
                for d, pre in enumerate(turns):
                    for m in range(MT):
                        act.wait_ge(u_projected, d * MT + m + 1)
                        nc.scalar.activation(up[:, m, :, NCONV - 1:NCONV - 1 + S],
                                             wide[:, m, :].rearrange("p (b s) -> p b s", s=S), ACT.Copy
                                             ).then_inc(u_copied, 1)
                    for m in range(MT):
                        act.wait_ge(z_projected, d * MT + m + 1)
                        bank = (bS[:, :], bO[:, :], bT[:, 0, :], bT[:, 1, :])[m]
                        if d:
                            act.wait_ge(y_ready, d)
                        nc.scalar.activation(zg[:, m, :], bank, ACT.Copy).then_inc(zg_ready, 1)
                        nc.scalar.activation(dtz[:, m, :], bank, ACT.Sigmoid).then_inc(zg_ready, 1)
                    act.wait_ge(conv_done, (d + 1) * MT)
                    nc.scalar.activation(u[:, :, :], tmp[:, :, :], ACT.Sigmoid).then_inc(u_ready, 1)
                    act.wait_ge(dbc_projected, d + 1)
                    nc.scalar.activation(dbc[:, :], bS[0:R, :], ACT.Copy).then_inc(dbc_ready, 1)
                    act.wait_ge(u_ready, 2 * d + 2)
                    bias = at[pre + "dt_b"]
                    for m in range(MT):
                        act.wait_ge(dt_projected, d * MT + m + 1)
                        nc.scalar.activation(tmp[:, m, :], wide[:, m, :], ACT.Identity,
                                             bias=w[:, bias + m:bias + m + 1]).then_inc(dt_logs_ready, 1)
                        nc.scalar.activation(dt[:, m, :], wide[:, m, :], ACT.Abs,
                                             bias=w[:, bias + m:bias + m + 1]).then_inc(dt_logs_ready, 1)
                    for m in range(MT):
                        act.wait_ge(dt_logs_ready, 4 * MT * d + 2 * m + 2)
                        nc.scalar.activation(dt[:, m, :], dt[:, m, :], ACT.Exp, scale=-1.0
                                             ).then_inc(dt_logs_ready, 1)
                    for m in range(MT):
                        act.wait_ge(dt_logs_ready, 4 * MT * d + 2 * MT + m + 1)
                        nc.scalar.activation(dt[:, m, :], dt[:, m, :], ACT.Ln, bias=1.0
                                             ).then_inc(dt_logs_ready, 1)
                    al = w[:, at[pre + "Alog"]:at[pre + "Alog"] + MT * NSTATE].rearrange("p (m n) -> p m n", m=MT)
                    nc.scalar.activation(A[:, :, :], al, ACT.Exp).then_inc(A_exp_ready, 1)
                    act.wait_ge(dt_ready, 4 * d + 4)
                    base = d * NSTATE
                    with act.Fori(0, NSTATE // 2) as i:
                        for j in range(2):
                            n = base + 2 * i + j
                            act.wait_ge(bc_done, n + 1)
                            act.wait_ge(y_added, n + d)
                            nc.scalar.activation(bc[:, j, 0, :], bS[:, :], ACT.Copy).then_inc(bc_ready, 1)
                            nc.scalar.activation(bc[:, j, 1, :], bO[:, :], ACT.Copy).then_inc(bc_ready, 1)
                            for m in range(MT):
                                nc.scalar.activation(dA[:, j, m, :], dtz[:, m, :], ACT.Exp,
                                                     scale=A[:, m, bass.ds(2 * i + j, 1)]).then_inc(dA_ready, 1)
                    if d == 1:
                        act.wait_ge(out_projected, 2)
                        nc.scalar.activation(ytok[:, :, :], bT[:, :, :].rearrange("p a (b n) -> p (a b) n", n=D),
                                             ACT.Copy).then_inc(ytok_ready, 1)

            @block.gpsimd
            def _(pool):
                for d, pre in enumerate(turns):
                    for m in range(MT):
                        pool.wait_ge(zg_ready, 3 * MT * d + 2 * MT)
                        nc.gpsimd.tensor_tensor(zg[:, m, :], zg[:, m, :], dtz[:, m, :], ALU.mult
                                                ).then_inc(zg_ready, 1)
                    pool.wait_ge(dbc_ready, d + 1)
                    pool.wait_ge(dt_ready, 4 * d + 4)
                    base = d * NSTATE

                    def rows(state, first=False):
                        if not (d == 0 and first):
                            pool.wait_ge(bc_done, base + state)
                        for c in range(2):
                            sel = L.const[0:R, bass.ds(C_IDENT + b_row + c * NSTATE + state, 1)]
                            nc.gpsimd.tensor_tensor(row[:, c, :], dbc[:, :], sel.broadcast_to([R, N]), ALU.mult
                                                    ).then_inc(row_ready, 1)

                    def state_input(i, j):
                        pool.wait_ge(bc_ready, 2 * (base + 2 * i + j) + 1)
                        nc.gpsimd.tensor_tensor(dBu[:, j, :, :], du[:, :, :],
                                                bc[:, j, 0, :].unsqueeze(1).broadcast_to([P, MT, N]),
                                                ALU.mult).then_inc(dBu_ready, 1)
                    rows(0, first=True)
                    with pool.Fori(0, NSTATE // 2 - 1) as i:
                        for j in range(2):
                            rows(2 * i + j + 1)
                            state_input(i, j)
                    rows(NSTATE - 1)
                    state_input(NSTATE // 2 - 1, 0)
                    state_input(NSTATE // 2 - 1, 1)

            @block.tensor
            def _(pe):
                pe.wait_ge(w_ready[0], w_ready[1])
                pe.wait_ge(z_ready, 2 if twice else 1)
                turn_tensor(L, wide, z=z2).then_inc(zT_turned, 1)
                pe.wait_ge(zT_ready, KT)
                if twice:
                    turn_tensor(L, wide, z=z2, flip=True).then_inc(zT_turned, 1)
                    pe.wait_ge(zT_ready, 2 * KT)
                for d, pre in enumerate(turns):
                    src = zT2 if d else L.zT
                    wi = w[:, at[pre + "in_w"]:at[pre + "in_w"] + KT * 2 * DI].rearrange("p (k n) -> p k n", k=KT)
                    wx = w[:, at[pre + "xproj"]:at[pre + "xproj"] + MT * R].rearrange("p (k n) -> p k n", k=MT)
                    wd = w[0:R, at[pre + "dt_w"]:at[pre + "dt_w"] + DI]
                    wo = w[:, at[pre + "out_w"]:at[pre + "out_w"] + MT * D].rearrange("p (k n) -> p k n", k=MT)
                    if d:
                        pe.wait_ge(y_ready, d)
                        pe.wait_ge(x_added, 1)
                    for n in range(2):
                        for m in range(MT):
                            out = wide[:, m, :] if n == 0 else (bS[:, :], bO[:, :], bT[:, 0, :], bT[:, 1, :])[m]
                            c = n * DI + m * P
                            for k in range(KT):
                                last = nc.tensor.matmul(out, wi[:, k, c:c + P], src[:, k, :],
                                                        start=(k == 0), stop=(k == KT - 1))
                            last.then_inc((u_projected, z_projected)[n], 1)
                    pe.wait_ge(u_ready, 2 * d + 2)
                    pe.wait_ge(zg_ready, 3 * MT * d + 2 * MT)
                    for m in range(MT):
                        last = nc.tensor.matmul(bS[0:R, :], wx[:, m, :], u[:, m, :], start=(m == 0), stop=(m == MT - 1))
                    last.then_inc(dbc_projected, 1)
                    pe.wait_ge(dbc_ready, d + 1)
                    pe.wait_ge(u_copied, (d + 1) * MT)
                    for m in range(MT):
                        nc.tensor.matmul(wide[:, m, :], wd[:, m * P:(m + 1) * P], dbc[:, :], start=True, stop=True
                                         ).then_inc(dt_projected, 1)
                    pe.wait_ge(uD_ready, (d + 1) * MT)
                    for m in range(MT):
                        last = nc.tensor.matmul(wide[:, m, :], L.ident, tmp[:, m, :], start=True, stop=True)
                    last.then_inc(y_added, 1)
                    base = d * NSTATE

                    def spread(n):
                        pe.wait_ge(row_ready, 2 * n + 2)
                        nc.tensor.matmul(bS[:, :], ones[:, :], row[:, 0, :], start=True, stop=True)
                        nc.tensor.matmul(bO[:, :], ones[:, :], row[:, 1, :], start=True, stop=True
                                         ).then_inc(bc_done, 1)

                    def add_state(n, j):
                        pe.wait_ge(hC_ready, n + 1)
                        for m in range(MT):
                            last = nc.tensor.matmul(wide[:, m, :], L.ident, dBu[:, j, m, :], start=False,
                                                    stop=True, skip_group_check=True)
                        last.then_inc(y_added, 1)

                    def step(n, j):
                        pe.wait_ge(bc_ready, 2 * n + 2)
                        spread(n + 1)
                        add_state(n, j)
                    if d:
                        pe.wait_ge(bc_ready, 2 * base)
                    spread(base)
                    with pe.Fori(0, NSTATE // 2 - 1) as i:
                        for j in range(2):
                            step(base + 2 * i + j, j)
                    step(base + NSTATE - 2, 0)
                    add_state(base + NSTATE - 1, 1)
                    pe.wait_ge(y_ready, d + 1)
                    for t in range(NT):
                        for m in range(MT):
                            last = nc.tensor.matmul(bT[:, t // 2, (t % 2) * D:(t % 2 + 1) * D],
                                                    tmp[:, m, t * P:(t + 1) * P], wo[:, m, :],
                                                    start=(m == 0), stop=(m == MT - 1))
                    last.then_inc(out_projected, 1)
                    if d:
                        pe.wait_ge(ytok_ready, 1)
                        for t in range(NT):
                            last = nc.tensor.matmul(bT[:, t // 2, (t % 2) * D:(t % 2 + 1) * D], L.flip, ytok[:, t, :],
                                                    start=True, stop=True)
                        last.then_inc(out_projected, 1)
        end_layer(nc, sems)


E = 8
C_TRI = 0


def gate_vector(L, nc, dve, chain, T, logit_ps, bias, kind, sel_bias, gate_shifted, gate_exp_ready):
    lg, ex, pr, m4, r4, mx8, ix8, ixf, oh, comb = T
    b8 = lambda a: a.unsqueeze(2).broadcast_to([P, NT, E])
    ps = logit_ps.rearrange("p (t e) -> p t e", e=E)
    iota = L.const[:, C_IOTA:C_IOTA + E].unsqueeze(1).broadcast_to([P, NT, E])
    if bias is not None:
        chain(nc.vector.tensor_tensor(lg[:, :, :], ps, bias.unsqueeze(1).broadcast_to([P, NT, E]), ALU.add))
    else:
        chain(nc.vector.tensor_copy(lg[:, :, :], ps))
    chain(nc.vector.tensor_reduce(m4[:, :], lg[:, :, :], AX.X, ALU.max))
    nc.vector.tensor_tensor(ex[:, :, :], lg[:, :, :], b8(m4[:, :]), ALU.subtract).then_inc(gate_shifted, 1)
    dve.wait_ge(gate_exp_ready, 1)
    chain(nc.vector.tensor_reduce(r4[:, :], ex[:, :, :], AX.X, ALU.add))
    chain(nc.vector.reciprocal(r4[:, :], r4[:, :]))
    chain(nc.vector.tensor_tensor(pr[:, :, :], ex[:, :, :], b8(r4[:, :]), ALU.mult))
    sel = lg if kind == "renormalised" else pr
    if sel_bias is not None:
        chain(nc.vector.tensor_tensor(lg[:, :, :], pr[:, :, :],
                                      sel_bias.unsqueeze(1).broadcast_to([P, NT, E]), ALU.add))
        sel = lg
    for t in range(NT):
        last = nc.vector.max(mx8[:, t, :], sel[:, t, :])
    chain(last)
    for t in range(NT):
        last = nc.vector.max_index(ix8[:, t, :], mx8[:, t, :], sel[:, t, :])
    chain(last)
    chain(nc.vector.tensor_copy(ixf[:, :, :], ix8[:, :, :]))
    chain(nc.vector.tensor_tensor(oh[:, :, :], iota, b8(ixf[:, :, 0]), ALU.is_equal))
    if kind == "switch":
        return
    chain(nc.vector.tensor_tensor(comb[:, :, :], iota, b8(ixf[:, :, 1]), ALU.is_equal))
    chain(nc.vector.tensor_tensor(oh[:, :, :], oh[:, :, :], comb[:, :, :], ALU.add))
    if kind == "renormalised":
        chain(nc.vector.tensor_tensor(comb[:, :, :], ex[:, :, :], oh[:, :, :], ALU.mult))
        chain(nc.vector.tensor_reduce(r4[:, :], comb[:, :, :], AX.X, ALU.add))
        chain(nc.vector.reciprocal(r4[:, :], r4[:, :]))
        chain(nc.vector.tensor_tensor(comb[:, :, :], comb[:, :, :], b8(r4[:, :]), ALU.mult))
    else:
        chain(nc.vector.tensor_tensor(comb[:, :, :], pr[:, :, :], oh[:, :, :], ALU.mult))


def experts(L, nc, name, w, at, w_ready, kind, src, F, norm=True, swiglu=False, linear=False, sel_bias=False):
    n_exp = src.shape[0]
    cols = src.shape[2]
    MF = F // P
    with ExitStack() as ctx:
        sems = []

        def sb(n, shape, dt=F32):
            return ctx.enter_context(nc.sbuf_tensor(name + n, shape, dt))

        def sem(n):
            s = ctx.enter_context(nc.semaphore(name + n))
            sems.append(s)
            return s
        wide, bS, bO, bT = psum4(nc, ctx, name)
        yps = bT[:, :, :].rearrange("p a (b n) -> p (a b) n", n=D)
        g3 = lambda n, dt=F32: sb(n, [P, NT, E], dt)
        T = (g3("logits"), g3("exp"), g3("probs"), sb("max", [P, NT]), sb("rsum", [P, NT]), g3("top"),
             g3("top_index", U32), g3("top_index_f"), g3("chosen"), sb("combine", [P, NT, E + 1]))
        comb_all = T[9]
        comb = comb_all[:, :, 0:E]
        T = T[:9] + (comb,)
        combe = sb("combine_e", [P, 1, NT])
        combT = sb("combineT", [E, NT, P])
        wb = sb("expert_w", [P, 2, cols])
        hT = sb("hidden", [P, MF, N])
        if swiglu:
            lin = sb("w1_part", [P, 2, N])
            gl = sb("gate_linear", [P, 2, 2, N])
            sg = sb("sigmoid", [P, 2, N])
        if kind == "switch":
            kept = sb("kept", [P, NT, E])
            keptf = sb("kept_any", [P, NT])
        dve_chain = sem("dve_chain")
        act_chain = sem("act_chain")
        ln_stats_ready = sem("ln_stats_ready")
        rstd_ready = sem("rstd_ready")
        z_ready = sem("z_ready")
        zT_turned = sem("zT_turned")
        zT_ready = sem("zT_ready")
        logits_ready = sem("logits_ready")
        gate_shifted = sem("gate_shifted")
        gate_exp_ready = sem("gate_exp_ready")
        onehot_ready = sem("onehot_ready")
        counted = sem("counted")
        comb_ready = sem("comb_ready")
        combT_turned = sem("combT_turned")
        combT_ready = sem("combT_ready")
        expert_loaded = [sem("expert_loaded_0"), sem("expert_loaded_1")]
        hidden_projected = sem("hidden_projected")
        hidden_ready = sem("hidden_ready")
        lin_ready = sem("lin_ready")
        pair_taken = sem("pair_taken")
        gl_ready = sem("gl_ready")
        sig_ready = sem("sig_ready")
        y_done = sem("y_done")
        y_taken = sem("y_taken")
        bias_done = sem("bias_done")
        nx = 1 if norm else 0
        turned_again = 1 if kind == "switch" else 0
        o2 = 0 if linear else (2 if swiglu else 1) * KT * (2 * F if swiglu else F)
        slots = [(wide[:, 0, :], wide[:, 1, :]), (wide[:, 2, :], wide[:, 3, :]), (bS[:, :], bO[:, :])]

        with nc.Block() as block:
            @block.sync
            def _(sp):
                for j in range(2):
                    sp.dma_start(wb[:, j, :], src[j]).then_inc(expert_loaded[j], 16)
                with sp.Fori(0, n_exp // 2 - 1) as i:
                    for j in range(2):
                        sp.wait_ge(y_done, 2 * i + j + 1)
                        sp.dma_start(wb[:, j, :], src[bass.ds(2 * i + 2 + j, 1)].squeeze(0)
                                     ).then_inc(expert_loaded[j], 16)
                if n_exp % 2:
                    sp.wait_ge(y_done, n_exp - 2)
                    sp.dma_start(wb[:, 0, :], src[n_exp - 1]).then_inc(expert_loaded[0], 16)

            @block.vector
            def _(dve):
                chain = Chain(dve, dve_chain)
                if norm:
                    norm_vector(L, dve, chain, ln_stats_ready, rstd_ready, z_ready)
                    dve.wait_ge(zT_turned, 1)
                    nc.vector.tensor_copy(L.zT[:, 1, :], wide[:, 1, :]).then_inc(zT_ready, 1)
                dve.wait_ge(logits_ready, 1)
                bias = w[:, at["br"]:at["br"] + E] if "br" in at else None
                gate_vector(L, nc, dve, chain, T, bS[:, 0:NT * E], bias, kind,
                            w[:, at["gate_b"]:at["gate_b"] + E] if sel_bias else None,
                            gate_shifted, gate_exp_ready)
                if n_exp > E:
                    chain(nc.vector.memset(comb_all[:, :, E:E + 1], 1.0))
                if kind == "switch":
                    nc.vector.tensor_copy(kept[:, :, :], T[8][:, :, :]).then_inc(onehot_ready, 1)
                    dve.wait_ge(counted, 1)
                    cnt = bO[:, 0:NT * E].rearrange("p (t e) -> p t e", e=E)
                    chain(nc.vector.scalar_tensor_tensor(kept[:, :, :], cnt, float(N // E), T[8][:, :, :],
                                                         ALU.is_lt, ALU.mult))
                    chain(nc.vector.tensor_reduce(keptf[:, :], kept[:, :, :], AX.X, ALU.add))
                    chain(nc.vector.tensor_tensor(keptf[:, :], keptf[:, :], T[5][:, :, 0], ALU.mult))
                    chain(nc.vector.tensor_tensor(comb, kept[:, :, :],
                                                  keptf[:, :].unsqueeze(2).broadcast_to([P, NT, E]), ALU.mult))
                    for t in range(NT):
                        last = nc.vector.tensor_scalar(L.z[:, t, :], L.z[:, t, :], keptf[:, t:t + 1], None,
                                                       ALU.mult)
                    last.then_inc(z_ready, 1)
                    dve.wait_ge(zT_turned, nx + 1)
                    nc.vector.tensor_copy(L.zT[:, 1, :], wide[:, 1, :]).then_inc(zT_ready, 1)
                chain(nc.vector.tensor_copy(combe[:, 0, :], comb[:, :, 0]))
                nc.vector.tensor_copy(combe[:, 0, :], comb[:, :, 0]).then_inc(comb_ready, 1)
                dve.wait_ge(comb_ready, 1)
                dve.wait_ge(combT_turned, 1)
                nc.vector.tensor_copy(combT[:, :, :], bS[0:E, :].rearrange("p (t n) -> p t n", n=P)
                                      ).then_inc(combT_ready, 1)

                def swiglu_part(e):
                    for m in range(MF):
                        for gl_n in range(2):
                            pair = 2 * m + gl_n
                            dve.wait_ge(lin_ready, e * 2 * MF + pair + 1)
                            b3 = at_b3 + gl_n * MF + m
                            nc.vector.scalar_tensor_tensor(
                                gl[:, m % 2, gl_n, :], slots[pair % 3][1], wb[:, e_j, b3:b3 + 1],
                                lin[:, pair % 2, :], ALU.add, ALU.mult).then_inc(pair_taken, 1)
                        dve.wait_ge(pair_taken, e * 2 * MF + 2 * m + 1)
                        nc.vector.tensor_scalar(gl[:, m % 2, 0, :], gl[:, m % 2, 0, :], 7.0, None, ALU.min
                                                ).then_inc(gl_ready, 1)
                        dve.wait_ge(pair_taken, e * 2 * MF + 2 * m + 2)
                        chain(nc.vector.tensor_scalar(gl[:, m % 2, 1, :], gl[:, m % 2, 1, :], 7.0, -7.0,
                                                      ALU.min, ALU.max))
                        dve.wait_ge(sig_ready, e * MF + m + 1)
                        chain(nc.vector.tensor_tensor(sg[:, m % 2, :], sg[:, m % 2, :], gl[:, m % 2, 0, :],
                                                      ALU.mult))
                        nc.vector.scalar_tensor_tensor(hT[:, m, :], gl[:, m % 2, 1, :], 1.0, sg[:, m % 2, :],
                                                       ALU.add, ALU.mult).then_inc(hidden_ready, 1)

                def expert(e):
                    if swiglu:
                        swiglu_part(e)
                    chain(nc.vector.tensor_copy(combe[:, 0, :].unsqueeze(2),
                                                comb_all[:, :, bass.ds(e, 1)]))
                    dve.wait_ge(y_done, e + 1)
                    for t in range(NT):
                        last = nc.vector.scalar_tensor_tensor(L.x[:, t, :], yps[:, t, :], combe[:, 0, t:t + 1],
                                                              L.x[:, t, :], ALU.mult, ALU.add)
                    last.then_inc(y_taken, 1)
                    dve.wait_ge(y_taken, e + 1)
                per = 1 + (2 * MF if swiglu else 0)
                at_b3 = cols - MF * 2
                with dve.Fori(0, n_exp // 2) as i:
                    with chain.loop(i, n_exp // 2, 2 * per):
                        for e_j in range(2):
                            expert(2 * i + e_j)
                if n_exp % 2:
                    e_j = 0
                    expert(n_exp - 1)
                dve.wait_ge(bias_done, 1)
                chain(nc.vector.tensor_tensor(L.x[:, :, :], L.x[:, :, :],
                                              wide[:, 0:2, :].rearrange("p a (b n) -> p (a b) n", n=D), ALU.add))

            @block.scalar
            def _(act):
                if norm:
                    norm_scalar(L, act, ln_stats_ready, rstd_ready)
                    act.wait_ge(zT_turned, 1)
                    nc.scalar.activation(L.zT[:, 0, :], wide[:, 0, :], ACT.Copy).then_inc(zT_ready, 1)
                act.wait_ge(gate_shifted, 1)
                nc.scalar.activation(T[1][:, :, :], T[1][:, :, :], ACT.Exp).then_inc(gate_exp_ready, 1)
                if kind == "switch":
                    act.wait_ge(zT_turned, nx + 1)
                    nc.scalar.activation(L.zT[:, 0, :], wide[:, 0, :], ACT.Copy).then_inc(zT_ready, 1)

                def relu_part(e, e_j):
                    for m in range(MF):
                        act.wait_ge(hidden_projected, e * MF + m + 1)
                        b1 = cols - MF + m
                        nc.scalar.activation(hT[:, m, :], wide[:, m % 4, :], ACT.Relu,
                                             bias=wb[:, e_j, b1:b1 + 1]).then_inc(hidden_ready, 1)

                def swiglu_part(e, e_j):
                    def sig(m):
                        act.wait_ge(gl_ready, e * MF + m + 1)
                        nc.scalar.activation(sg[:, m % 2, :], gl[:, m % 2, 0, :], ACT.Sigmoid, scale=1.702
                                             ).then_inc(sig_ready, 1)
                    for m in range(MF):
                        for gl_n in range(2):
                            pair = 2 * m + gl_n
                            act.wait_ge(hidden_projected, e * 2 * MF + pair + 1)
                            if pair >= 2:
                                act.wait_ge(pair_taken, e * 2 * MF + pair - 1)
                            b1 = cols - 4 * MF + gl_n * MF + m
                            nc.scalar.activation(lin[:, pair % 2, :], slots[pair % 3][0], ACT.Identity,
                                                 bias=wb[:, e_j, b1:b1 + 1]).then_inc(lin_ready, 1)
                        sig(m)
                part = swiglu_part if swiglu else relu_part
                if not linear:
                    with act.Fori(0, n_exp // 2) as i:
                        for e_j in range(2):
                            part(2 * i + e_j, e_j)
                    if n_exp % 2:
                        part(n_exp - 1, 0)

            @block.tensor
            def _(pe):
                if norm:
                    pe.wait_ge(z_ready, 1)
                    turn_tensor(L, wide).then_inc(zT_turned, 1)
                    pe.wait_ge(zT_ready, 2)
                pe.wait_ge(w_ready[0], w_ready[1])
                wr = w[:, at["Wr"]:at["Wr"] + KT * E].rearrange("p (k n) -> p k n", k=KT)
                for t in range(NT):
                    for k in range(KT):
                        last = nc.tensor.matmul(bS[:, t * E:(t + 1) * E], L.zT[:, k, t * P:(t + 1) * P],
                                                wr[:, k, :], start=(k == 0), stop=(k == KT - 1))
                last.then_inc(logits_ready, 1)
                if kind == "switch":
                    tri = w[:, at["tri"]:at["tri"] + 2 * P]
                    pe.wait_ge(onehot_ready, 1)
                    for t in range(NT):
                        for u in range(t + 1):
                            m = tri[:, 0:P] if u == t else tri[:, P:2 * P]
                            last = nc.tensor.matmul(bO[:, t * E:(t + 1) * E], m, T[8][:, u, :],
                                                    start=(u == 0), stop=(u == t))
                    last.then_inc(counted, 1)
                    pe.wait_ge(z_ready, nx + 1)
                    turn_tensor(L, wide).then_inc(zT_turned, 1)
                    pe.wait_ge(zT_ready, 2 * nx + 2)
                pe.wait_ge(comb_ready, 1)
                for t in range(NT):
                    last = nc.tensor.transpose(bS[0:E, t * P:(t + 1) * P], comb[:, t, :], L.ident)
                last.then_inc(combT_turned, 1)
                pe.wait_ge(combT_ready, 1)

                def expert(e, e_j, loaded):
                    pe.wait_ge(expert_loaded[e_j], loaded)
                    wv = wb[:, e_j, :]
                    for m in range(0 if linear else MF):
                        if swiglu:
                            for gl_n in range(2):
                                pair = 2 * m + gl_n
                                if pair >= 3:
                                    pe.wait_ge(pair_taken, e * 2 * MF + pair - 2)
                                for a in range(2):
                                    o = a * KT * 2 * F
                                    w1 = wv[:, o:o + KT * 2 * F].rearrange("p (k n) -> p k n", k=KT)
                                    c = gl_n * F + m * P
                                    for k in range(KT):
                                        last = nc.tensor.matmul(slots[pair % 3][a], w1[:, k, c:c + P],
                                                                L.zT[:, k, :], start=(k == 0), stop=(k == KT - 1))
                                last.then_inc(hidden_projected, 1)
                            continue
                        if m >= 4:
                            pe.wait_ge(hidden_ready, e * MF + m - 3)
                        w1 = wv[:, 0:KT * F].rearrange("p (k n) -> p k n", k=KT)
                        for k in range(KT):
                            last = nc.tensor.matmul(wide[:, m % 4, :], w1[:, k, m * P:(m + 1) * P],
                                                    L.zT[:, k, :], start=(k == 0), stop=(k == KT - 1))
                        last.then_inc(hidden_projected, 1)
                    pe.wait_ge(y_taken, e)
                    n_k = KT if linear else MF
                    w2 = wv[:, o2:o2 + n_k * D].rearrange("p (k n) -> p k n", k=n_k)
                    if not linear:
                        pe.wait_ge(hidden_ready, e * MF + MF)
                    hs = L.zT if linear else hT
                    for t in range(NT):
                        for k in range(n_k):
                            last = nc.tensor.matmul(yps[:, t, :], hs[:, k, t * P:(t + 1) * P], w2[:, k, :],
                                                    start=(k == 0), stop=(k == n_k - 1))
                    last.then_inc(y_done, 1)
                with pe.Fori(0, n_exp // 2) as i:
                    for e_j in range(2):
                        expert(2 * i + e_j, e_j, 16 * i + 16)
                if n_exp % 2:
                    expert(n_exp - 1, 0, 16 * (n_exp // 2) + 16)
                b2 = w[0:E, at["b2"]:at["b2"] + D]
                n_b = 2 if n_exp > E else 1
                for t in range(NT):
                    out = wide[:, t // 2, (t % 2) * D:(t % 2 + 1) * D]
                    last = nc.tensor.matmul(out, combT[:, t, :], b2, start=True, stop=(n_b == 1))
                    if n_b == 2:
                        last = nc.tensor.matmul(out, w[0:1, at["one"]:at["one"] + P],
                                                w[0:1, at["sb2"]:at["sb2"] + D], start=False, stop=True)
                last.then_inc(bias_done, 1)
        end_layer(nc, sems)


class Pack:
    def __init__(self):
        self.at, self.n, self.parts = {}, 0, []

    def add(self, name, cols, make):
        self.at[name] = self.n
        self.n += cols
        self.parts.append(make)

    def array(self, i):
        return np.ascontiguousarray(np.concatenate([f(i) for f in self.parts], axis=1))


def pack_l0_attn():
    k = Pack()
    for n in ("Wq", "Wk", "Wv", "Wo"):
        k.add(n, KT * D, lambda i, n=n: _rows(i["L0_attn_" + n]))
    for n in ("bq", "bk"):
        k.add(n, KT, lambda i, n=n: _col(i["L0_attn_" + n]))
    for n in ("bv", "bo"):
        k.add(n, D, lambda i, n=n: _bc(i["L0_attn_" + n]))
    return k


def pack_l3_attn():
    k = Pack()
    spread = lambda w: np.repeat(w.reshape(D, 4, 1, HD), 4, axis=2).reshape(D, D)
    k.add("Wq", KT * D, lambda i: _rows(i["L3_attn_Wq"]))
    k.add("Wk", KT * D, lambda i: _rows(spread(i["L3_attn_Wk"])))
    k.add("Wv", KT * D, lambda i: _rows(spread(i["L3_attn_Wv"])))
    k.add("Wo", KT * D, lambda i: _rows(i["L3_attn_Wo"]))
    return k


def l0_attn(L, nc, w, w_ready, at):
    mask = L.const[:, C_CAUSAL:C_CAUSAL + S].unsqueeze(1).broadcast_to([P, NP_, S])
    self_attention(L, nc, "L0_attn_", w, [at[n] for n in ("Wq", "Wk", "Wv", "Wo")], HD ** -0.5,
                   [at[n] for n in ("bq", "bk", "bv", "bo")], mask, None, w_ready)


def l3_attn(L, nc, w, w_ready, at):
    mask = L.const[:, C_ALIBI:C_ALIBI + NP_ * S].rearrange("p (a s) -> p a s", s=S)
    self_attention(L, nc, "L3_attn_", w, [at[n] for n in ("Wq", "Wk", "Wv", "Wo")], HD ** -0.5,
                   None, mask, None, w_ready)



def _experts(parts):
    out = []
    for e in range(parts[0].shape[0]):
        out.append(np.concatenate([_rows(p[e]) if p.ndim == 3 else _col(p[e]) for p in parts], axis=1))
    return np.ascontiguousarray(np.stack(out))


def pack_l0_ffn():
    k = Pack()
    k.add("Wr", KT * E, lambda i: _rows(i["L0_ffn_Wr"]))
    k.add("br", E, lambda i: _bc(i["L0_ffn_br"]))
    k.add("b2", D, lambda i: _pad(i["L0_ffn_b2"]))
    k.add("tri", 2 * P, lambda i: np.concatenate([np.triu(np.ones((P, P), np.float32)),
                                                  np.ones((P, P), np.float32)], axis=1))
    return k


def l0_ffn(L, nc, w, w_ready, at):
    experts(L, nc, "L0_ffn_", w, at, w_ready, "switch", L.aps["x_L0_ffn"], D)


def pack_l1_ffn():
    k = Pack()
    k.add("Wr", KT * E, lambda i: _rows(i["L1_ffn_gate_w"].T))
    k.add("gate_b", E, lambda i: _bc(i["L1_ffn_gate_b"]))
    k.add("b2", D, lambda i: _pad(i["L1_ffn_b2"]))
    k.add("sb2", D, lambda i: _pad(i["L1_ffn_sb2"].reshape(1, D)))
    k.add("one", P, lambda i: np.ones((P, P), np.float32))
    return k


def l1_ffn(L, nc, w, w_ready, at):
    experts(L, nc, "L1_ffn_", w, at, w_ready, "top2", L.aps["x_L1_ffn"], 512, swiglu=True, sel_bias=True)


def pack_l2_ffn():
    k = Pack()
    k.add("Wr", KT * E, lambda i: _rows(i["L2_ffn_Wr"]))
    k.add("br", E, lambda i: _bc(i["L2_ffn_br"]))
    k.add("b2", D, lambda i: _pad(i["L2_ffn_b2"]))
    return k


def l2_ffn(L, nc, w, w_ready, at):
    experts(L, nc, "L2_ffn_", w, at, w_ready, "renormalised", L.aps["x_L2_ffn"], 1024)


def pack_l3_ffn():
    k = Pack()
    third = lambda i, n: _rows(i["L3_ffn_W_qkv"][:, n * D:(n + 1) * D])
    for n, name in enumerate(("Wq", "Wk", "Wv")):
        k.add(name, KT * D, lambda i, n=n: third(i, n))
    k.add("Wo", KT * D, lambda i: _rows(np.eye(D, dtype=np.float32)))
    for n, name in enumerate(("bq", "bk")):
        k.add(name, KT, lambda i, n=n: _col(i["L3_ffn_b_qkv"][n * D:(n + 1) * D]))
    k.add("bv", D, lambda i: _bc(i["L3_ffn_b_qkv"][2 * D:]))
    k.add("no_mask", S, lambda i: np.zeros((P, S), np.float32))
    k.add("Wr", KT * E, lambda i: _rows(i["L3_ffn_W_gate"]))
    k.add("br", E, lambda i: _bc(i["L3_ffn_b_gate"]))
    k.add("b2", D, lambda i: _pad(i["L3_ffn_b_experts"]))
    return k


def l3_ffn(L, nc, w, w_ready, at):
    mask = w[:, at["no_mask"]:at["no_mask"] + S].unsqueeze(1).broadcast_to([P, NP_, S])
    self_attention(L, nc, "L3_ffn_", w, [at[n] for n in ("Wq", "Wk", "Wv", "Wo")], HD ** -0.5,
                   [at["bq"], at["bk"], at["bv"], None], mask, None, w_ready)
    experts(L, nc, "L3_moe_", w, at, w_ready, "top2", L.aps["x_L3_ffn"], D, norm=False, linear=True)


def expert_arrays(i, layers):
    out = {}
    if "L0_ffn" in layers:
        out["x_L0_ffn"] = _experts([i["L0_ffn_W1"], i["L0_ffn_W2"], i["L0_ffn_b1"]])
    if "L1_ffn" in layers:
        turn = lambda a: np.concatenate([a[..., ::2], a[..., 1::2]], axis=-1)
        add = lambda n: np.concatenate([i["L1_ffn_" + n], i["L1_ffn_s" + n][None]], axis=0)
        out["x_L1_ffn"] = _experts([turn(add("w1")), turn(add("w3")), add("w2"), turn(add("b1")), turn(add("b3"))])
    if "L2_ffn" in layers:
        out["x_L2_ffn"] = _experts([i["L2_ffn_W1"], i["L2_ffn_W2"], i["L2_ffn_b1"]])
    if "L3_ffn" in layers:
        out["x_L3_ffn"] = _experts([i["L3_ffn_W_experts"]])
    return out


def pack_l2_xattn():
    k = Pack()
    k.add("Wq", KT * D, lambda i: _rows(i["L2_xattn_Wq"].T))
    k.add("Wk", KT * D, lambda i: _rows(i["L2_xattn_Wk"]))
    k.add("Wv", KT * D, lambda i: _rows(i["L2_xattn_Wv"].T))
    return k


def pack_l3_xattn():
    k = Pack()
    for n in ("Wq", "Wk", "Wv", "Wp"):
        k.add(n, KT * D, lambda i, n=n: _rows(i["L3_xattn_" + n].T))
    for n in ("bq", "bk", "bv", "bp"):
        k.add(n, D, lambda i, n=n: _bc(i["L3_xattn_" + n]))
    return k


def pack_l1_xattn():
    k = Pack()
    for n in ("wq", "wk", "wv", "wo"):
        k.add(n, KT * D, lambda i, n=n: _rows(i["L1_xattn_" + n]))
    for n in ("bq", "bk", "bv"):
        k.add(n, KT, lambda i, n=n: _col(i["L1_xattn_" + n]))
    k.add("bo", D, lambda i: _bc(i["L1_xattn_bo"]))
    return k


def pack_l1_attn():
    k = Pack()
    for n in ("ln_g", "ln_b"):
        k.add(n, KT, lambda i, n=n: _col(i["L1_attn_" + n]))
    DI, R, MT = 512, 96, 4
    for pre in ("f_", "b_"):
        g = lambda i, n, pre=pre: i["L1_attn_" + pre + n]
        k.add(pre + "in_w", KT * 2 * DI, lambda i, g=g: _rows(g(i, "in_w").T))
        k.add(pre + "xproj", MT * R, lambda i, g=g: _rows(g(i, "xproj_w").T))
        k.add(pre + "dt_w", DI, lambda i, g=g: _pad(np.ascontiguousarray(g(i, "dt_w").T)))
        k.add(pre + "out_w", MT * D, lambda i, g=g: _rows(g(i, "out_w").T))
        k.add(pre + "conv_w", MT * NCONV, lambda i, g=g: _rows(g(i, "conv_w")))
        for n in ("conv_b", "dt_b", "D"):
            k.add(pre + n, MT, lambda i, g=g, n=n: _col(g(i, n)))
        k.add(pre + "Alog", MT * NSTATE, lambda i, g=g: _rows(g(i, "Alog")))
    return k


def l1_attn(L, nc, w, w_ready, at):
    mamba(L, nc, "L1_attn_", w, at, w_ready, 512, 96, 64, ("f_", "b_"), True)


def pack_l2_attn():
    k = Pack()
    g = lambda i, n: i["L2_attn_" + n]
    DI, R, MT = 256, 33, 2
    k.add("in_w", KT * 2 * DI, lambda i: _rows(g(i, "in_proj_w").T))
    k.add("xproj", MT * R, lambda i: _rows(g(i, "x_proj_w").T))
    k.add("dt_w", DI, lambda i: np.where(np.arange(P)[:, None] == 32, 1.0, 0.0).astype(np.float32)
          * np.ones((1, DI), np.float32))
    k.add("out_w", MT * D, lambda i: _rows(g(i, "out_proj_w").T))
    k.add("conv_w", MT * NCONV, lambda i: _rows(g(i, "conv_w")))
    k.add("conv_b", MT, lambda i: _col(g(i, "conv_b")))
    k.add("dt_b", MT, lambda i: np.zeros((P, MT), np.float32))
    k.add("D", MT, lambda i: _col(g(i, "D_param")))
    k.add("Alog", MT * NSTATE, lambda i: _rows(g(i, "A_log")))
    return k


def l2_attn(L, nc, w, w_ready, at):
    mamba(L, nc, "L2_attn_", w, at, w_ready, 256, 33, 0, ("",), False)


def pack_l0_xattn():
    k = Pack()
    g = lambda i, n: i["L0_xattn_" + n]
    k.add("Wq", KT * 1024, lambda i: _rows(g(i, "Wq")))
    k.add("Wk", KT * 1024, lambda i: _rows(g(i, "Wkv")[:, :1024]))
    k.add("Wv", KT * 1024, lambda i: _rows(g(i, "Wkv")[:, 1024:]))
    k.add("Wout", 8 * D, lambda i: _rows(g(i, "Wout")))
    for n in ("ln_x_g", "ln_x_b", "ln_l_g", "ln_l_b", "bout"):
        k.add(n, D, lambda i, n=n: _bc(g(i, n)))
    for n in ("qn_g", "kn_g"):
        k.add(n, 1, lambda i, n=n: np.concatenate([g(i, n), g(i, n)]).reshape(P, 1))
    return k


LAYERS = [("L0_xattn", pack_l0_xattn, l0_xattn), ("L0_attn", pack_l0_attn, l0_attn), ("L0_ffn", pack_l0_ffn, l0_ffn),
          ("L1_xattn", pack_l1_xattn, l1_xattn), ("L1_attn", pack_l1_attn, l1_attn),
          ("L1_ffn", pack_l1_ffn, l1_ffn), ("L2_xattn", pack_l2_xattn, l2_xattn), ("L2_attn", pack_l2_attn, l2_attn),
          ("L2_ffn", pack_l2_ffn, l2_ffn), ("L3_xattn", pack_l3_xattn, l3_xattn),
          ("L3_attn", pack_l3_attn, l3_attn), ("L3_ffn", pack_l3_ffn, l3_ffn)]
RAW = ["ctx_tok", "ctx_feat"]


def program(nc, aps, out, layers):
    with ExitStack() as ctx:
        L = Layer(nc, ctx, aps)
        x_loaded = ctx.enter_context(nc.semaphore("x_loaded"))
        weights_loaded = [ctx.enter_context(nc.semaphore(f"weights_loaded_{n}")) for n in range(2)]
        out_stored = ctx.enter_context(nc.semaphore("out_stored"))
        packs = [(name, make(), run) for name, make, run in LAYERS if name in layers]

        def load_weights(eng, n):
            cols = packs[n][1].n
            eng.dma_start(L.weights[n % 2][:, 0:cols], aps["w_" + packs[n][0]]).then_inc(weights_loaded[n % 2], 16)

        with nc.Block() as block:
            @block.sync
            def _(sp):
                sp.dma_start(L.x[:, :, :], aps["x"].rearrange("(t p) d -> p t d", p=P)).then_inc(x_loaded, 16)
                sp.dma_start(L.const[:, :], aps["const"]).then_inc(x_loaded, 16)
                load_weights(sp, 0)
                sp.wait_ge(x_loaded, 32)
        for n, (name, pack, run) in enumerate(packs):
            if n + 1 < len(packs):
                with nc.Block() as block:
                    @block.sync
                    def _(sp):
                        load_weights(sp, n + 1)
            run(L, nc, L.weights[n % 2], (weights_loaded[n % 2], 16 * (n // 2 + 1)), pack.at)
        with nc.Block() as block:
            @block.sync
            def _(sp):
                sp.dma_start(out.rearrange("(t p) d -> p t d", p=P), L.x[:, :, :]).then_inc(out_stored, 16)
                sp.wait_ge(out_stored, 16)


def kernel(_layers=None, **inputs):
    import concourse.bacc as _bacc
    from concourse.bass_utils import run_bass_kernel_spmd as _run

    layers = _layers or [n for n, _, _ in LAYERS]
    i = {k: np.asarray(v) for k, v in inputs.items()}
    arrays = {"x": np.ascontiguousarray(i["x"].reshape(N, D)), "const": constants()}
    for name, make, _ in LAYERS:
        if name in layers:
            arrays["w_" + name] = make().array(i)
    arrays.update(extra_arrays(i))
    arrays.update(expert_arrays(i, layers))
    nc = _bacc.Bacc("TRN2", target_bir_lowering=False, num_devices=1)
    aps = {n: nc.dram_tensor("in_" + n, a.shape, mybir.dt.from_np(a.dtype), kind="ExternalInput").ap()
           for n, a in arrays.items()}
    out = nc.dram_tensor("out_x", (N, D), F32, kind="ExternalOutput").ap()
    program(nc, aps, out, layers)
    r = _run(nc, [{"in_" + n: a for n, a in arrays.items()}], core_ids=[0])
    return r.results[0]["out_x"].reshape(B, S, D)


def extra_arrays(i):
    ctx = i["ctx_1024"]
    return {"mask_BSS2": i["mask_BxSxS2_ff0"], "mask_SS2": i["mask_1x1xSxS2_fk1"].reshape(S, CTX),
            "mask_BS2": i["mask_BxS2_bf1"].view(np.uint8),
            "ctx_tok": np.ascontiguousarray(ctx), "ctx_feat": np.ascontiguousarray(ctx.transpose(0, 2, 1))}
```
